# Optimizing a Trainium2 kernel written in Bass

```python
import numpy as np
import jax
import jax.numpy as jnp

def _softmax(x, axis=-1):
    return jax.nn.softmax(x, axis=axis)

def _gelu(x):
    return jax.nn.gelu(x, approximate=True)

def _silu(x):
    return jax.nn.silu(x)

def _sigmoid(x):
    return jax.nn.sigmoid(x)

def _layernorm(x, axis=-1, eps=1e-05):
    m = jnp.mean(x, axis=axis, keepdims=True)
    v = jnp.var(x, axis=axis, keepdims=True)
    return (x - m) / jnp.sqrt(v + eps)

def _scatter_add(tgt, idx, src, axis=0):
    return tgt.at[idx].add(src)

def _segment_sum(src, seg, n):
    return jax.ops.segment_sum(src, seg, n)
kernel_name = 'mk_cond_resid_d4_seqx_r8_c07b4d'

def setup_inputs(seed: int=0):
    np.random.seed(seed)
    _w = jnp.asarray

    def _rec_inputs():
        import jax
        import jax.numpy as jnp
        _rk = jax.random.key(seed)
        x = -7.109e-05 + 0.9999 * jax.random.normal(jax.random.fold_in(_rk, 1), (32, 32, 256), jnp.float32)
        _lenS = 32 - jax.random.randint(jax.random.fold_in(_rk, 7), (32,), 0, max(1, 32 // 4) + 1, jnp.int32)
        _lenS2 = 32 - jax.random.randint(jax.random.fold_in(_rk, 8), (32,), 0, max(1, 32 // 4) + 1, jnp.int32)
        itok_B_1_198 = jax.random.randint(jax.random.fold_in(_rk, 11), (32,), 1, 199, jnp.int32)
        itok_B_0_6 = jax.random.randint(jax.random.fold_in(_rk, 12), (32,), 0, 7, jnp.int32)
        itok_Bx257_0_4111 = jax.random.randint(jax.random.fold_in(_rk, 13), (32, 257), 0, 514, jnp.int32)
        itok_B_37_3939 = jax.random.randint(jax.random.fold_in(_rk, 14), (32,), 37, 3940, jnp.int32)
        itok_B_0_15 = jax.random.randint(jax.random.fold_in(_rk, 15), (32,), 0, 16, jnp.int32)
        return (x, itok_B_1_198, itok_B_0_6, itok_Bx257_0_4111, itok_B_37_3939, itok_B_0_15)
    x, itok_B_1_198, itok_B_0_6, itok_Bx257_0_4111, itok_B_37_3939, itok_B_0_15 = _rec_inputs()

    def _L0_cond_setup():
        import jax, jax.numpy as jnp
        import numpy as np
        B, C, T = (128, 32, 256)
        S, D = (200, 32)
        key = jax.random.key(seed)
        k1, k2, k3 = jax.random.split(key, 3)
        x = jax.random.normal(k1, (B, C, T), dtype=jnp.float32)
        conditions = jax.random.randint(k2, (B,), 0, S, dtype=jnp.int64)
        weights = jax.random.normal(k3, (S, C, D), dtype=jnp.float32) / jnp.sqrt(jnp.float32(C))
        return {'x': x, 'conditions': conditions, 'weights': weights}
    _L0_cond_all = _L0_cond_setup()
    _L0_cond_in = {k: v for k, v in _L0_cond_all.items() if k in ('weights',)}
    del _L0_cond_all

    def _L1_cond_setup():
        import jax, jax.numpy as jnp
        import numpy as np
        B, T, D_IN, D_OUT = (16, 256, 256, 256)
        N_ADAPTERS, RANK = (8, 16)
        key = jax.random.key(seed)
        k_x, k_w, k_a, k_b, k_s, k_idx = jax.random.split(key, 6)
        x = jax.random.normal(k_x, (B, T, D_IN), dtype=jnp.float32)
        W = jax.random.normal(k_w, (D_OUT, D_IN), dtype=jnp.float32) * (1.0 / np.sqrt(D_IN))
        A = jax.random.normal(k_a, (N_ADAPTERS, RANK, D_IN), dtype=jnp.float32) * 0.02
        Bm = jax.random.normal(k_b, (N_ADAPTERS, D_OUT, RANK), dtype=jnp.float32) * 0.02
        scalings = jnp.ones((N_ADAPTERS,), dtype=jnp.float32)
        adapter_idx = jax.random.randint(k_idx, (B,), 0, N_ADAPTERS, dtype=jnp.int32)
        return {'x': x, 'W': W, 'A': A, 'Bm': Bm, 'scalings': scalings, 'adapter_idx': adapter_idx}
    _L1_cond_all = _L1_cond_setup()
    _L1_cond_in = {k: v for k, v in _L1_cond_all.items() if k in ('W', 'A', 'Bm', 'scalings')}
    del _L1_cond_all

    def _L2_cond_setup():
        import jax, jax.numpy as jnp
        import numpy as np
        H, G, HD = (8, 4, 32)
        GSZ = H // G
        BLOCK = 16
        WINDOW = 128
        SCALE = 256.0 ** (-0.5)
        EPS = 1e-06
        THETA = 10000.0
        B, T, D = (16, 4, 256)
        NBLK = 257

        def _rms(x, scale):
            var = jnp.mean(x * x, axis=-1, keepdims=True)
            return x * jax.lax.rsqrt(var + EPS) * (1.0 + scale)

        def _rope(x, pos):
            half = HD // 2
            inv = 1.0 / THETA ** (jnp.arange(half, dtype=jnp.float32) / half)
            ang = pos[:, :, None].astype(jnp.float32) * inv
            cos = jnp.cos(ang)[:, None, :, :]
            sin = jnp.sin(ang)[:, None, :, :]
            x1, x2 = (x[..., :half], x[..., half:])
            return jnp.concatenate([x1 * cos - x2 * sin, x2 * cos + x1 * sin], axis=-1)
        key = jax.random.key(seed)
        ks = jax.random.split(key, 10)
        inv_d = 1.0 / np.sqrt(D)
        return {'x': jax.random.normal(ks[0], (B, T, D), jnp.float32), 'Wq': jax.random.normal(ks[1], (H * HD, D), jnp.float32) * inv_d, 'Wk': jax.random.normal(ks[2], (G * HD, D), jnp.float32) * inv_d, 'Wv': jax.random.normal(ks[3], (G * HD, D), jnp.float32) * inv_d, 'Wo': jax.random.normal(ks[4], (D, H * HD), jnp.float32) * inv_d, 'q_norm_scale': jax.random.normal(ks[5], (HD,), jnp.float32) * 0.02, 'k_norm_scale': jax.random.normal(ks[6], (HD,), jnp.float32) * 0.02, 'k_blocks': jax.random.normal(ks[7], (B * NBLK, G, BLOCK, HD), jnp.float32), 'v_blocks': jax.random.normal(ks[8], (B * NBLK, G, BLOCK, HD), jnp.float32), 'block_tables': jnp.arange(B * NBLK, dtype=jnp.int32).reshape(B, NBLK), 'kv_lens': jax.random.randint(ks[9], (B,), 0, 512, dtype=jnp.int32)}
    _L2_cond_all = _L2_cond_setup()
    _L2_cond_in = {k: v for k, v in _L2_cond_all.items() if k in ('Wq', 'Wk', 'Wv', 'Wo', 'q_norm_scale', 'k_norm_scale', 'k_blocks', 'v_blocks')}
    del _L2_cond_all

    def _L3_cond_setup():
        import jax, jax.numpy as jnp
        import numpy as np
        key = jax.random.key(seed)
        k1, k2, k3, k4 = jax.random.split(key, 4)
        B, S, IN, OUT, E = (64, 32, 256, 256, 16)
        bound = 1.0 / np.sqrt(IN)
        x = jax.random.normal(k1, (B, S, IN), dtype=jnp.float32)
        idx = jax.random.randint(k2, (B,), 0, E, dtype=jnp.int64)
        W = jax.random.uniform(k3, (E, IN, OUT), dtype=jnp.float32, minval=-bound, maxval=bound)
        b = jnp.full((E, OUT), 0.1, dtype=jnp.float32)
        return {'x': x, 'id': idx, 'W': W, 'b': b}
    _L3_cond_all = _L3_cond_setup()
    _L3_cond_in = {k: v for k, v in _L3_cond_all.items() if k in ('W', 'b')}
    del _L3_cond_all
    return {'x': x, 'itok_B_1_198': itok_B_1_198, 'itok_B_0_6': itok_B_0_6, 'itok_Bx257_0_4111': itok_Bx257_0_4111, 'itok_B_37_3939': itok_B_37_3939, 'itok_B_0_15': itok_B_0_15, 'L0_cond_weights': _L0_cond_in['weights'], 'L1_cond_W': _L1_cond_in['W'], 'L1_cond_A': _L1_cond_in['A'], 'L1_cond_Bm': _L1_cond_in['Bm'], 'L1_cond_scalings': _L1_cond_in['scalings'], 'L2_cond_Wq': _L2_cond_in['Wq'], 'L2_cond_Wk': _L2_cond_in['Wk'], 'L2_cond_Wv': _L2_cond_in['Wv'], 'L2_cond_Wo': _L2_cond_in['Wo'], 'L2_cond_q_norm_scale': _L2_cond_in['q_norm_scale'], 'L2_cond_k_norm_scale': _L2_cond_in['k_norm_scale'], 'L2_cond_k_blocks': _L2_cond_in['k_blocks'], 'L2_cond_v_blocks': _L2_cond_in['v_blocks'], 'L3_cond_W': _L3_cond_in['W'], 'L3_cond_b': _L3_cond_in['b']}

def reference(x, itok_B_1_198, itok_B_0_6, itok_Bx257_0_4111, itok_B_37_3939, itok_B_0_15, L0_cond_weights, L1_cond_W, L1_cond_A, L1_cond_Bm, L1_cond_scalings, L2_cond_Wq, L2_cond_Wk, L2_cond_Wv, L2_cond_Wo, L2_cond_q_norm_scale, L2_cond_k_norm_scale, L2_cond_k_blocks, L2_cond_v_blocks, L3_cond_W, L3_cond_b):
    import jax
    import jax.numpy as jnp

    def _L0_cond_ref(x, conditions, weights):
        import jax, jax.numpy as jnp
        import numpy as np
        B, C, T = (128, 32, 256)
        S, D = (200, 32)
        w = weights[conditions]
        return jnp.einsum('bct,bcd->bdt', x, w)

    def _L1_cond_ref(x, W, A, Bm, scalings, adapter_idx):
        import jax, jax.numpy as jnp
        import numpy as np
        B, T, D_IN, D_OUT = (16, 256, 256, 256)
        N_ADAPTERS, RANK = (8, 16)
        H = jnp.einsum('btd,od->bto', x, W)
        A_b = A[adapter_idx]
        B_b = Bm[adapter_idx]
        s_b = scalings[adapter_idx]
        xa = jnp.einsum('btd,brd->btr', x, A_b)
        delta = jnp.einsum('btr,bor->bto', xa, B_b)
        delta = jax.lax.stop_gradient(delta * s_b[:, None, None])
        return H + delta

    def _L2_cond_ref(x, Wq, Wk, Wv, Wo, q_norm_scale, k_norm_scale, k_blocks, v_blocks, block_tables, kv_lens):
        import jax, jax.numpy as jnp
        import numpy as np
        H, G, HD = (8, 4, 32)
        GSZ = H // G
        BLOCK = 16
        WINDOW = 128
        SCALE = 256.0 ** (-0.5)
        EPS = 1e-06
        THETA = 10000.0
        B, T, D = (16, 4, 256)
        NBLK = 257

        def _rms(x, scale):
            var = jnp.mean(x * x, axis=-1, keepdims=True)
            return x * jax.lax.rsqrt(var + EPS) * (1.0 + scale)

        def _rope(x, pos):
            half = HD // 2
            inv = 1.0 / THETA ** (jnp.arange(half, dtype=jnp.float32) / half)
            ang = pos[:, :, None].astype(jnp.float32) * inv
            cos = jnp.cos(ang)[:, None, :, :]
            sin = jnp.sin(ang)[:, None, :, :]
            x1, x2 = (x[..., :half], x[..., half:])
            return jnp.concatenate([x1 * cos - x2 * sin, x2 * cos + x1 * sin], axis=-1)
        Bx, Tx, _ = x.shape
        q = jnp.einsum('btd,od->bto', x, Wq).reshape(Bx, Tx, H, HD).transpose(0, 2, 1, 3)
        k = jnp.einsum('btd,od->bto', x, Wk).reshape(Bx, Tx, G, HD).transpose(0, 2, 1, 3)
        v = jnp.einsum('btd,od->bto', x, Wv).reshape(Bx, Tx, G, HD).transpose(0, 2, 1, 3)
        q = _rms(q, q_norm_scale)
        k = _rms(k, k_norm_scale)
        pos = kv_lens[:, None] + jnp.arange(Tx, dtype=jnp.int32)
        q = _rope(q, pos)
        k = _rope(k, pos)
        slot = pos // BLOCK
        off = pos % BLOCK
        blk = jnp.take_along_axis(block_tables, slot, axis=1)
        k_blocks = k_blocks.at[blk, :, off, :].set(k.transpose(0, 2, 1, 3))
        v_blocks = v_blocks.at[blk, :, off, :].set(v.transpose(0, 2, 1, 3))
        k_all = k_blocks[block_tables].transpose(0, 2, 1, 3, 4).reshape(Bx, G, -1, HD)
        v_all = v_blocks[block_tables].transpose(0, 2, 1, 3, 4).reshape(Bx, G, -1, HD)
        S = k_all.shape[2]
        qg = q.reshape(Bx, G, GSZ, Tx, HD)
        scores = jnp.einsum('bghtd,bgsd->bghts', qg, k_all) * SCALE
        kpos = jnp.arange(S, dtype=jnp.int32)
        allowed = (kpos[None, None, :] <= pos[:, :, None]) & (kpos[None, None, :] > pos[:, :, None] - WINDOW)
        scores = jnp.where(allowed[:, None, None, :, :], scores, -jnp.inf)
        p = jax.nn.softmax(scores, axis=-1)
        o = jnp.einsum('bghts,bgsd->bghtd', p, v_all).reshape(Bx, H, Tx, HD)
        o = o.transpose(0, 2, 1, 3).reshape(Bx, Tx, H * HD)
        return jnp.einsum('bto,do->btd', o, Wo)

    def _L3_cond_ref(x, id, W, b):
        import jax, jax.numpy as jnp
        import numpy as np
        Wg = W[id]
        bg = b[id]
        out = jnp.einsum('bsi,bio->bso', x, Wg) + bg[:, None, :]
        return out
    x = x + _L0_cond_ref(x, itok_B_1_198, L0_cond_weights)
    x = x + _L1_cond_ref(x, L1_cond_W, L1_cond_A, L1_cond_Bm, L1_cond_scalings, itok_B_0_6)
    x = x + _L2_cond_ref(x, L2_cond_Wq, L2_cond_Wk, L2_cond_Wv, L2_cond_Wo, L2_cond_q_norm_scale, L2_cond_k_norm_scale, L2_cond_k_blocks, L2_cond_v_blocks, itok_Bx257_0_4111, itok_B_37_3939)
    x = x + _L3_cond_ref(x, itok_B_0_15, L3_cond_W, L3_cond_b)
    return x

_drawn_inputs = setup_inputs


def setup_inputs(seed=0):
    import zlib

    import numpy as np

    out = dict(_drawn_inputs(seed))
    spreads = {'L1_cond_scalings': (1.0, 0.6), 'L3_cond_b': (0.10000000149011612, 0.6)}
    factors = {'L1_cond_A': 3.232,
     'L1_cond_Bm': 3.229,
     'L2_cond_Wk': 65.17,
     'L2_cond_q_norm_scale': 8.0,
     'L2_cond_k_norm_scale': 200.0,
     'L2_cond_k_blocks': 4.153}
    for name, (base, spread) in spreads.items():
        noise = np.random.default_rng([zlib.crc32(name.encode()), seed]).standard_normal(out[name].shape)
        drawn = base * np.exp(spread * noise) if base else spread * noise
        out[name] = jnp.asarray(drawn.astype(out[name].dtype))
    for name, factor in factors.items():
        out[name] = (out[name] * factor).astype(out[name].dtype)
    return out
```

```python
from contextlib import ExitStack

import numpy as np

import concourse.bass as bass
from concourse import mybir
from concourse.alu_op_type import AluOpType as ALU

ACT = mybir.ActivationFunctionType
AX = mybir.AxisListType
F32 = mybir.dt.float32
BF16 = mybir.dt.bfloat16
I32 = mybir.dt.int32

P = 128
B, T, D = 32, 32, 256
KC = D // P
B4 = P // T
NT = B // B4
H, G, HD = 8, 4, 32
GS = H // G
KV = G * HD
BLOCK, WINDOW, NBLK = 16, 128, 257
SLOTS = 257
NPOOL = 16 * NBLK
SCALE = float(D) ** -0.5
EPS = 1e-6
THETA = 10000.0
ADAPTERS, RANK = 8, 16
EXPERTS = 16
NCOND = 200
KEYS = 160
KB = KEYS - P
WB = 11
WROWS = WB * BLOCK
SEQ_U = 11
UNITS = [(0, 11), (11, 11), (22, 10)]
NW = 3
NWI = B * NW
NEW0 = 0
WIN0 = NEW0 + B * T
NROWS = WIN0 + B * WROWS
BIG = 1e30
TWO_PI_HI = 6.28125
TWO_PI_MID = 0.0019350051879882812
TWO_PI_LO = 2 * np.pi - TWO_PI_HI - TWO_PI_MID
ROUND = 12582912.0
PI_SAFE = 3.1415925


class Columns:

    def __init__(self):
        p = np.arange(P)
        r = lambda a: np.broadcast_to(np.asarray(a, np.float32), (P, len(a)))
        c = lambda a: np.asarray(a, np.float32).reshape(P, -1)
        half = HD // 2
        inv = (np.float32(1.0) / np.power(np.float32(THETA), np.arange(half, dtype=np.float32) / np.float32(half)))
        parts = {
            "ident": np.eye(P),
            "iota": r(np.arange(KEYS)),
            "inv": r(inv.astype(np.float32)),
            "quad": c([[q // T == j for j in range(B4)] for q in p]),
            "in_tile": c(p % T),
            "unit_seq": c([[q // WB == j for j in range(SEQ_U)] for q in p]),
            "unit_blk": c(p % WB),
            "unit_row": c([[min(u * SEQ_U + q // WB, B - 1) * SLOTS for u in range(3)] for q in p]),
            "wr_seq": c([[q // NW == j for j in range(B)] for q in p]),
            "wr_blk": c(p % NW),
            "wr_row": c(np.minimum(p // NW, B - 1) * SLOTS),
            "wr_off": c([[BLOCK * (q % NW) + o for o in range(BLOCK)] for q in p]),
            "wr_new": c(p // NW * T + NEW0 + 1),
            "later": c([[i < q for i in range(NWI)] for q in p]),
            "win_row": c([[WIN0 + q * WROWS + x + 1 for x in range(WROWS)] for q in p]),
            "adapter": c(p // RANK),
        }
        self.at, self.data, n = {}, [], 0
        for k, v in parts.items():
            v = np.asarray(v, np.float32)
            self.at[k] = (n, n + v.shape[1])
            self.data.append(v)
            n += v.shape[1]
        self.width = n
        self.data = np.ascontiguousarray(np.concatenate(self.data, 1), np.float32)


def program(nc, x, cond, adapter_idx, table, kv_lens, expert_ids, W0, W1, A1, B1, s1, Wq, Wk, Wv, Wo, q_norm, k_norm,
            k_blocks, v_blocks, W3, b3, consts, out):
    cols = Columns()
    ctx = ExitStack()

    def sb(name, shape, dt=F32):
        return ctx.enter_context(nc.sbuf_tensor(name, shape, dt))

    def sem(name):
        return ctx.enter_context(nc.semaphore(name))

    with ctx:
        kv_rows = nc.dram_tensor("kv_rows", [NROWS, 2 * KV], F32).ap()

        cst = sb("cst", [P, cols.width])

        def C(name, parts=P, a=0, b=None):
            lo, hi = cols.at[name]
            return cst[0:parts, lo + a:(hi if b is None else lo + b)]

        ident = C("ident")
        ones = sb("ones", [P, P])
        nat = sb("nat", [P, 2, 4, D])
        natA = sb("natA", [P, D])
        natB = sb("natB", [P, KC, P])
        W1T = sb("W1T", [P, KC, D])
        WkvT = sb("WkvT", [P, KC, 2 * KV])
        WqT = sb("WqT", [P, KC, GS, KV])
        WoT = sb("WoT", [P, GS, D])
        AT = sb("AT", [P, KC, P])
        BT = sb("BT", [P, D])
        xin = sb("xin", [P, NT, D])
        mixw = sb("mixw", [P, NT, T])
        mix = sb("mix", [P, NT, P])
        x1T = sb("x1T", [P, KC, B * T])
        qn = x1T[:, :, :].rearrange("p c r -> p (c r)").rearrange("p (n c) -> p n c", n=NT)
        x2T = sb("x2T", [P, KC, B * T])
        xaT = sb("xaT", [P, B * T])
        kvn = sb("kvn", [P, NT, 2 * KV])
        tmp = sb("tmp", [P, 2, 2 * 256])
        tmp2 = sb("tmp2", [P, 2, 2 * 256])
        ssq = sb("ssq", [P, NT, H])
        rstd = sb("rstd", [P, NT, H])
        ssk = sb("ssk", [P, NT, G])
        rstdk = sb("rstdk", [P, NT, G])
        eps = sb("eps", [P, 1])
        blk = sb("blk", [P, 3, BLOCK * KV])
        blkp = sb("blkp", [P, 2, BLOCK * KV])
        lens_i = sb("lens_i", [P, B + 1], I32)
        cond_i = sb("cond_i", [P, B], I32)
        adp_i = sb("adp_i", [P, B], I32)
        ids_i = sb("ids_i", [1, B], I32)
        lens = sb("lens", [P, B + 1])
        condf = sb("condf", [P, B])
        first = sb("first", [P, B + 1])
        first_i = sb("first_i", [P, B + 1], I32)
        slot_i = sb("slot_i", [P, 4, B + 1], I32)
        slot = sb("slot", [P, 4, B + 1])
        sel = sb("sel", [P, 4, B + 1])
        pick = sb("pick", [P, 8])
        tidx = sb("tidx", [P, 4])
        tidx_i = sb("tidx_i", [P, 4], I32)
        tab_i = sb("tab_i", [P, 4], I32)
        tab = sb("tab", [P, 4])
        mixi = sb("mixi", [P, NT])
        mixi_i = sb("mixi_i", [P, NT], I32)
        diag = sb("diag", [P, 4, P])
        hit = sb("hit", [P, B * WB])
        later = sb("later", [P, NWI])
        wr = sb("wr", [P, 4, BLOCK])
        bits_i = sb("bits_i", [P, 4], I32)
        bits = sb("bits", [P, 4])
        rows = sb("rows", [B, 3, WROWS])
        rowA = sb("rowA", [P, B], I32)
        rowB = sb("rowB", [P, NT], I32)
        scal = sb("scal", [P, 1])
        amask = sb("amask", [P, B])
        pos = sb("pos", [P, NT])
        ang = sb("ang", [P, NT, 2, HD // 2])
        turns = sb("turns", [P, NT, 2, HD // 2])
        trig = sb("trig", [P, NT, 2, HD // 2])
        ns = sb("ns", [P, 2, 2, HD])
        rot = sb("rot", [P, 2, 2, NT, HD])
        hi = sb("hi", [P, B])
        sel8 = sb("sel8", [P, NT, B4])
        mask = sb("mask", [P, B, KEYS], BF16)
        NA = 16
        kvA = sb("kvA", [P, NA, 2 * KV])
        kvB = sb("kvB", [P, 3, 2 * KV])
        VBD = xin[:, 0:4, :].rearrange("p n c -> p (n c)").rearrange("p (g b c) -> p g b c", g=2, b=B4)
        KT = sb("KT", [P, 2, B4, KEYS])
        QBD = sb("QBD", [P, 2, B4, G, GS * T])
        S = sb("S", [P, 2, 2, KEYS])
        pr = sb("pr", [P, 2, 2, B4, KEYS])
        prB = sb("prB", [P, 2, 2, B4, KB])
        mx = sb("mx", [P, 4, 2])
        nb = sb("nb", [P, 4, 2])
        rs = sb("rs", [P, 8, 2])
        ri = sb("ri", [P, 8, 2])
        PTA = sb("PTA", [P, 3, 2, P])
        PTB = sb("PTB", [P, 2, 2, P])
        oT = sb("oT", [P, 2, B4, GS, T])
        x3T = sb("x3T", [P, 2, KC, P])
        NE = 4
        We = sb("We", [P, NE, KC, D])
        be = sb("be", [P, 2, D])
        res = nat[:, :, 0, :]
        bank = [ctx.enter_context(nc.psum_tensor(f"bank{i}", [P, 512], F32)) for i in range(8)]

        s_cst, s_lens, s_cond, s_adp, s_ids, s_x = (sem(f"{n}_loaded") for n in ("cst", "lens", "cond", "adp", "ids", "x"))
        s_scal, s_norms, s_wo_l = sem("scal_loaded"), sem("norms_loaded"), sem("wo_loaded")
        s_w1, s_ab, s_kvw, s_qw = sem("w1_loaded"), sem("ab_loaded"), sem("kvw_loaded"), sem("qw_loaded")
        s_set = sem("constants_set")
        s_ix = sem("index_step")
        s_mixi, s_tidx, s_mixw, s_tab = sem("mix_index_ready"), sem("table_index_ready"), sem("mix_weights_loaded"), sem("table_read")
        s_bl = [sem(f"blocks_loaded{i}") for i in range(3)]
        s_perm = sem("blocks_permuted")
        s_permA = sem("blocks_permuted_act")
        s_winw = [sem(f"window_written{i}") for i in range(2)]
        s_neww = sem("new_rows_written")
        s_diag, s_brd, s_inr, s_cnt, s_val, s_nrow, s_rowf, s_rowT, s_rowi = (
            sem(n) for n in ("diagonals_ready", "blocks_broadcast", "writers_ready", "overwrites_counted", "valid_ready",
                             "new_row_found", "key_rows_ready", "key_rows_turned", "key_rows_int"))
        s_wt, s_wtA, s_wtD = sem("weights_turned"), sem("weights_kept_act"), sem("weights_kept_dve")
        s_mix = sem("mix_ready")
        s_l0, s_x1A, s_x1D = sem("mix_done"), sem("x1_kept_act"), sem("x1_kept_dve")
        s_xa, s_xas, s_l1, s_x2 = sem("down_done"), sem("down_kept"), sem("layer1_done"), sem("x2_kept")
        s_am = sem("adapter_mask_ready")
        s_kvp, s_kvk, s_qp, s_qk = sem("kv_projected"), sem("kv_kept"), sem("q_projected"), sem("q_kept")
        s_an, s_tr, s_rt = sem("angles_ready"), sem("trig_ready"), sem("rotation_ready")
        s_sqr, s_ss, s_rt2, s_nstep, s_rot2, s_kready, s_qready = (
            sem(n) for n in ("squares_ready", "sums_ready", "roots_ready", "norm_step", "rotated_half", "k_ready", "q_ready"))
        s_hi, s_dist, s_mask = sem("middles_ready"), sem("distances_ready"), sem("masks_ready")
        dist = lambda g: pr[:, g % 2, 0, :, :]
        s_kvA = [sem(f"kvA_loaded{i}") for i in range(NA)]
        s_kvB = [sem(f"kvB_loaded{i}") for i in range(3)]
        s_kt, s_kta, s_ktb, s_qt = sem("k_turned"), sem("kA_kept"), sem("kB_kept"), sem("q_kept_diagonal")
        s_qz, s_vz, s_vbd = sem("q_diagonal_zeroed"), sem("v_diagonal_zeroed"), sem("v_diagonal_ready")
        s_sc, s_mx, s_nb, s_exp, s_ri, s_pn = (sem(n) for n in (
            "scores_ready", "max_ready", "bias_ready", "exp_ready", "inverse_ready", "probs_ready"))
        s_pt, s_pts, s_pv, s_ot = sem("probs_turned"), sem("probs_kept"), sem("pv_done"), sem("o_kept")
        s_wo, s_x3, s_l3, s_res = sem("wo_done"), sem("x3_kept"), sem("layer3_done"), sem("result_ready")
        s_we = [sem(f"expert_loaded{i}") for i in range(NE)]
        s_be = [sem(f"expert_bias_loaded{i}") for i in range(2)]
        s_out = [sem(f"output_written{i}") for i in range(2)]

        block = ctx.enter_context(nc.Block())

        pool_k = k_blocks.rearrange("n g o d -> n (g o d)")
        pool_v = v_blocks.rearrange("n g o d -> n (g o d)")
        LOADS = [(u, kv) for u in range(3) for kv in range(2)]
        PERM_BY_ACT = lambda i: i % 2 == 1
        out_rows = out.rearrange("b t d -> (b t) d").rearrange("(n p) d -> n p d", p=P)

        @block.sync
        def _(sp):
            sp.dma_start(lens_i[:, 0:B], kv_lens.partition_broadcast(P)).then_inc(s_lens, 16)
            sp.dma_start(cond_i[:, :], cond.partition_broadcast(P)).then_inc(s_cond, 16)
            sp.dma_start(cst[:, :], consts).then_inc(s_cst, 16)
            sp.dma_start(ids_i[:, :], expert_ids.unsqueeze(0)).then_inc(s_ids, 16)
            sp.dma_start(natA[:, :], A1.rearrange("n r d -> (n r) d")).then_inc(s_ab, 16)
            for oc in range(KC):
                sp.dma_start(natB[:, oc, :].rearrange("p (n r) -> p n r", r=RANK),
                             B1[:, oc * P:(oc + 1) * P, :].rearrange("n o r -> o n r")).then_inc(s_ab, 16)
            sp.dma_start(nat[:, 0, 2, :], Wk).then_inc(s_kvw, 16)
            sp.dma_start(nat[:, 1, 2, :], Wv).then_inc(s_kvw, 16)

            for i, (u, kv) in enumerate(LOADS):
                b0, nb_ = UNITS[u]
                n = nb_ * WB
                if PERM_BY_ACT(i):
                    sp.wait_ge(s_permA, i // 2 + 1)
                else:
                    sp.wait_ge(s_perm, i // 2 + 1)
                r0 = WIN0 + b0 * WROWS
                dst = kv_rows[r0:r0 + n * BLOCK, kv * KV:(kv + 1) * KV].rearrange("(p o) c -> p o c", o=BLOCK)
                sp.dma_start(dst, blkp[0:n, i % 2, :].rearrange("p (o c) -> p o c", o=BLOCK)).then_inc(s_winw[i % 2], 16)
            for t in range(NT // 2):
                sp.wait_ge(s_kready, t + 1)
                r0 = NEW0 + 2 * t * P
                sp.dma_start(kv_rows[r0:r0 + 2 * P, :].rearrange("(j p) c -> p j c", p=P),
                             kvn[:, 2 * t:2 * t + 2, :]).then_inc(s_neww, 16)
            sp.wait_ge(s_ids, 16)

            def expert(b):
                g = b // B4
                if b >= NE:
                    sp.wait_ge(s_l3, (b - NE) // B4 + 1)
                if g >= 2 and b % B4 == 0:
                    sp.wait_ge(s_res, g - 1)
                e = sp.value_load(ids_i[0:1, b:b + 1], min_val=0, max_val=EXPERTS - 1)
                sp.dma_start(We[:, b % NE, :, :], W3[bass.ds(e, 1), :, :].rearrange("e (c p) o -> p (e c) o", p=P)) \
                    .then_inc(s_we[b % NE], 16)
                sp.dma_start(be[T * (b % B4):T * (b % B4) + T, g % 2, :],
                             b3[bass.ds(e, 1), :].rearrange("e o -> (e o)").partition_broadcast(T)).then_inc(s_be[g % 2], 16)

            for b in range(NE):
                expert(b)
            nxt = NE
            for g in range(NT):
                while nxt < B and (nxt - NE) // B4 <= g and not (nxt % B4 == 0 and nxt // B4 - 1 > g):
                    expert(nxt)
                    nxt += 1
                sp.wait_ge(s_res, g + 1)
                sp.dma_start(out_rows[g], res[:, g % 2, :]).then_inc(s_out[g % 2], 16)
            assert nxt == B
            for j in range(2):
                sp.wait_ge(s_out[j], 16 * NT // 2)

        @block.gpsimd
        def _(pool):
            pool.memset(ones[:, :], 1.0).then_inc(s_set, 1)
            pool.memset(lens_i[:, B:B + 1], 0).then_inc(s_set, 1)
            pool.memset(eps[:, :], EPS).then_inc(s_set, 1)
            for j in range(2):
                pool.memset(QBD[:, j, :, :, :], 0.0).then_inc(s_qz, 1)
            pool.wait_ge(s_tidx, 1)
            table_1 = table.rearrange("b s -> (b s)").unsqueeze(1)
            for u in range(4):
                n = UNITS[u][1] * WB if u < 3 else NWI
                pool.indirect_dma_start(out=tab_i[0:n, u:u + 1], out_offset=None, in_=table_1,
                                        in_offset=bass.IndirectOffsetOnAxis(ap=tidx_i[0:n, u:u + 1], axis=0)).then_inc(s_tab, 16)
            pool.wait_ge(s_mixi, 1)
            W0_rows = W0.rearrange("s c d -> (s c) d")
            for t in range(NT):
                pool.indirect_dma_start(out=mixw[:, t, :], out_offset=None, in_=W0_rows,
                                        in_offset=bass.IndirectOffsetOnAxis(ap=mixi_i[:, t:t + 1], axis=0)).then_inc(s_mixw, 16)
            pool.wait_ge(s_tab, 64)
            for i, (u, kv) in enumerate(LOADS):
                n = UNITS[u][1] * WB
                if i >= 3:
                    j = i - 3
                    pool.wait_ge(s_permA if PERM_BY_ACT(j) else s_perm, j // 2 + 1)
                pool.indirect_dma_start(out=blk[0:n, i % 3, :], out_offset=None, in_=(pool_k, pool_v)[kv],
                                        in_offset=bass.IndirectOffsetOnAxis(ap=tab_i[0:n, u:u + 1], axis=0)).then_inc(s_bl[i % 3], 16)
            pool.wait_ge(s_l0, 4)
            pool.memset(VBD[:, :, :, :], 0.0).then_inc(s_vz, 1)
            pool.wait_ge(s_rowi, 5)
            for j in range(2):
                pool.wait_ge(s_winw[j], 48)
            pool.wait_ge(s_neww, 16 * NT // 2)
            for b in range(B):
                if b >= NA:
                    pool.wait_ge(s_pv, b - NA + 1)
                if b % B4 == 0:
                    g = b // B4
                    if g >= 3:
                        pool.wait_ge(s_pv, B4 * (g - 2))
                    pool.indirect_dma_start(out=kvB[:, g % 3, :], out_offset=None, in_=kv_rows,
                                            in_offset=bass.IndirectOffsetOnAxis(ap=rowB[:, g:g + 1], axis=0)).then_inc(s_kvB[g % 3], 16)
                pool.indirect_dma_start(out=kvA[:, b % NA, :], out_offset=None, in_=kv_rows,
                                        in_offset=bass.IndirectOffsetOnAxis(ap=rowA[:, b:b + 1], axis=0)).then_inc(s_kvA[b % NA], 16)

        @block.scalar
        def _(act):
            for j in range(NT // 4):
                act.dma_start(xin[:, 4 * j:4 * j + 4, :],
                              x.rearrange("b c t -> (b c) t").rearrange("(n p) t -> p n t", p=P)[:, 4 * j:4 * j + 4, :]) \
                    .then_inc(s_x, 16)
            act.dma_start(nat[:, :, 0, :], W1.rearrange("(c p) d -> p c d", p=P)).then_inc(s_w1, 16)
            act.dma_start(adp_i[:, :], adapter_idx.partition_broadcast(P)).then_inc(s_adp, 16)
            act.dma_start(scal[:, :], s1.unsqueeze(1).broadcast_to([ADAPTERS, RANK])).then_inc(s_scal, 16)
            for j, w in enumerate((q_norm, k_norm)):
                act.dma_start(ns[:, j, 0, :], w.partition_broadcast(P)).then_inc(s_norms, 16)
            act.dma_start(nat[:, :, 1, :], Wq.rearrange("(c p) d -> p c d", p=P)).then_inc(s_qw, 16)
            for oc in range(KC):
                for s in range(GS):
                    act.dma_start(nat[:, oc, 3, s * KV:(s + 1) * KV].rearrange("p (g d) -> p g d", g=G),
                                  Wo[oc * P:(oc + 1) * P, :].rearrange("p (g s d) -> p s g d", g=G, s=GS)[:, s]) \
                        .then_inc(s_wo_l, 16)

            for k, (src, dst) in enumerate(((0, W1T), (2, WkvT), (4, WoT))):
                act.wait_ge(s_wt, src + 1)
                act.copy(dst[:, :, :], bank[src][:, :].rearrange("p (c o) -> p c o", c=2)).then_inc(s_wtA, 1)
            def distances(g):
                if g == 0:
                    act.wait_ge(s_hi, 1)
                if g >= 2:
                    act.wait_ge(s_mask, g - 1)
                for j in range(B4):
                    act.activation(dist(g)[:, j, :], C("iota"), ACT.Square, bias=hi[:, B4 * g + j:B4 * g + j + 1]) \
                        .then_inc(s_dist, 1)

            distances(0)
            distances(1)
            act.wait_ge(s_an, 1)
            act.activation(trig[:, :, :, :], ang[:, :, :, :], ACT.Sin).then_inc(s_tr, 1)
            for h in range(2):
                act.wait_ge(s_l0, 2 * h + 1)
                act.copy(x1T[:, 0, 512 * h:512 * h + 512], bank[(5, 0)[h]][:, :]).then_inc(s_x1A, 1)

            def permute(i):
                n = UNITS[LOADS[i][0]][1] * WB
                act.wait_ge(s_bl[i % 3], 16 * (i // 3 + 1))
                if i >= 2:
                    act.wait_ge(s_winw[i % 2], 16 * (i // 2))
                act.copy(blkp[0:n, i % 2, :].rearrange("p (o g d) -> p g o d", o=BLOCK, g=G),
                         blk[0:n, i % 3, :].rearrange("p (g o d) -> p g o d", g=G, o=BLOCK)).then_inc(s_permA, 1)

            permute(1)
            permute(3)
            for t in range(NT // 2):
                act.wait_ge(s_kvp, t + 1)
                act.copy(kvn[:, 2 * t:2 * t + 2, :], bank[1 + t][:, :].rearrange("p (j c) -> p j c", j=2)).then_inc(s_kvk, 1)
            permute(5)
            for t in range(NT // 2):
                act.wait_ge(s_ss, t + 1)
                act.activation(rstdk[:, 2 * t:2 * t + 2, :], ssk[:, 2 * t:2 * t + 2, :], ACT.Sqrt,
                               bias=eps[:, 0:1], scale=1.0 / HD).then_inc(s_rt2, 1)
            for t in range(NT // 2):
                act.wait_ge(s_qp, t + 1)
                act.copy(qn[:, 2 * t:2 * t + 2, :], bank[(5, 6, 0, 7)[t]][:, :].rearrange("p (j c) -> p j c", j=2)).then_inc(s_qk, 1)
            for g in range(2, NT):
                distances(g)
            for t in range(NT // 2):
                act.wait_ge(s_ss, NT // 2 + t + 1)
                act.activation(rstd[:, 2 * t:2 * t + 2, :], ssq[:, 2 * t:2 * t + 2, :], ACT.Sqrt,
                               bias=eps[:, 0:1], scale=1.0 / HD).then_inc(s_rt2, 1)

            def keep_q(g):
                act.wait_ge(s_kt, 2 * g + 2)
                if g >= 2:
                    act.wait_ge(s_sc, B4 * (g - 1))
                act.copy(KT[:, g % 2, :, P:KEYS], bank[2][:, 0:P].rearrange("p (b r) -> p b r", b=B4)).then_inc(s_ktb, 1)
                if g == 0:
                    act.wait_ge(s_qz, 2)
                for k in range(G):
                    q = slice(HD * k, HD * k + HD)
                    act.copy(QBD[q, g % 2, :, k, :].rearrange("p b (s t) -> p s b t", s=GS),
                             bank[2][q, P:P + 2 * P].rearrange("p (s b t) -> p s b t", s=GS, b=B4)).then_inc(s_qt, 1)

            def keep_probs(seq):
                g, j = divmod(seq, B4 + 1)
                act.wait_ge(s_pt, seq + 1)
                if j == 0:
                    if g >= 2:
                        act.wait_ge(s_pv, B4 * (g - 1))
                    dst = PTB[:, g % 2, :, :]
                else:
                    m = B4 * g + j - 1
                    if m >= 3:
                        act.wait_ge(s_pv, m - 2)
                    dst = PTA[:, m % 3, :, :]
                act.copy(dst, bank[5 + seq % 2][:, 0:2 * P].rearrange("p (u r) -> p u r", u=2)).then_inc(s_pts, 1)

            keep_q(0)
            for n in range(B + B4):
                if n < B:
                    act.wait_ge(s_nb, n + 1)
                    if n >= 2 * B4:
                        act.wait_ge(s_pt, (n // B4 - 1) * (B4 + 1))
                    if n >= 8:
                        act.wait_ge(s_pn, 3 * (n - 7))
                    for u in range(2):
                        act.activation(pr[:, n // B4 % 2, u, n % B4, :], S[:, n % 2, u, :], ACT.Exp,
                                       bias=nb[:, n % 4, u:u + 1], scale=SCALE,
                                       accum_out=rs[:, n % 8, u:u + 1]).then_inc(s_exp, 1)
                if n % B4 == 2 and n // B4 + 1 < NT:
                    keep_q(n // B4 + 1)
                m = n - B4
                if m >= 0:
                    if m % B4 == 0:
                        keep_probs(m // B4 * (B4 + 1))
                    keep_probs(m // B4 * (B4 + 1) + m % B4 + 1)

        @block.vector
        def _(dve):
            ix = [0]

            def step(ins):
                ix[0] += 1
                ins.then_inc(s_ix, 1)
                dve.wait_ge(s_ix, ix[0])

            tt, ts, stt, cp = dve.tensor_tensor, dve.tensor_scalar, dve.scalar_tensor_tensor, dve.tensor_copy

            dve.wait_ge(s_lens, 16)
            dve.wait_ge(s_set, 3)
            step(cp(lens[:, :], lens_i[:, :]))
            step(ts(first[:, :], lens[:, :], float(WINDOW - 1), 0.0, ALU.subtract, ALU.max))
            step(cp(first_i[:, :], first[:, :]))
            ts(slot_i[:, 0, :], first_i[:, :], 4, None, ALU.arith_shift_right)
            ts(slot_i[:, 1, :], first_i[:, :], 15, None, ALU.bitwise_and)
            ts(slot_i[:, 2, :], lens_i[:, :], 4, None, ALU.arith_shift_right)
            step(ts(slot_i[:, 3, :], lens_i[:, :], 15, None, ALU.bitwise_and))
            step(cp(slot[:, :, :], slot_i[:, :, :]))
            dve.wait_ge(s_cst, 16)
            step(tt(sel[:, 0:3, 0:SEQ_U], slot[:, 0, :].rearrange("p (u b) -> p u b", b=SEQ_U),
                    C("unit_seq").unsqueeze(1).broadcast_to([P, 3, SEQ_U]), ALU.mult))
            dve.tensor_reduce(pick[:, 0:3], sel[:, 0:3, 0:SEQ_U], AX.X, ALU.add)
            step(tt(sel[:, 3, 0:B], slot[:, 2, 0:B], C("wr_seq"), ALU.mult))
            step(dve.tensor_reduce(pick[:, 3:4], sel[:, 3, 0:B], AX.X, ALU.add))
            ts(tidx[:, 0:3], pick[:, 0:3], C("unit_blk"), float(SLOTS - 1), ALU.add, ALU.min)
            step(ts(tidx[:, 3:4], pick[:, 3:4], C("wr_blk"), float(SLOTS - 1), ALU.add, ALU.min))
            tt(tidx_i[:, 0:3], tidx[:, 0:3], C("unit_row"), ALU.add)
            step(tt(tidx_i[:, 3:4], tidx[:, 3:4], C("wr_row"), ALU.add))
            dve.sem_inc(s_tidx, 1)

            dve.wait_ge(s_cond, 16)
            step(cp(condf[:, :], cond_i[:, :]))
            step(tt(sel8[:, :, :], condf[:, :].rearrange("p (n b) -> p n b", b=B4),
                    C("quad").unsqueeze(1).broadcast_to([P, NT, B4]), ALU.mult))
            step(dve.tensor_reduce(mixi[:, :], sel8[:, :, :], AX.X, ALU.add))
            ts(mixi_i[:, :], mixi[:, :], float(T), C("in_tile"), ALU.mult, ALU.add).then_inc(s_mixi, 1)

            step(tt(hi[:, :], lens[:, 0:B], first[:, 0:B], ALU.subtract))
            ts(hi[:, :], hi[:, :], -1.0, (WINDOW - 1) / 2, ALU.mult, ALU.add).then_inc(s_ix, 1)
            ix[0] += 1
            dve.wait_ge(s_ix, ix[0])
            ts(hi[:, :], hi[:, :], C("in_tile"), None, ALU.subtract).then_inc(s_hi, 1)

            step(tt(sel8[:, :, :], lens[:, 0:B].rearrange("p (n b) -> p n b", b=B4),
                    C("quad").unsqueeze(1).broadcast_to([P, NT, B4]), ALU.mult))
            step(dve.tensor_reduce(pos[:, :], sel8[:, :, :], AX.X, ALU.add))
            step(ts(pos[:, :], pos[:, :], C("in_tile"), None, ALU.add))
            for k in range(2):
                tt(ang[:, :, k, :], pos[:, :].unsqueeze(2).broadcast_to([P, NT, HD // 2]),
                   C("inv").unsqueeze(1).broadcast_to([P, NT, HD // 2]), ALU.mult).then_inc(s_ix, 1)
            ix[0] += 2
            dve.wait_ge(s_ix, ix[0])
            step(ts(turns[:, :, :, :], ang[:, :, :, :], float(1 / (2 * np.pi)), None, ALU.mult))
            step(ts(turns[:, :, 1, :], turns[:, :, 1, :], 0.25, None, ALU.add))
            step(ts(turns[:, :, :, :], turns[:, :, :, :], ROUND, None, ALU.add))
            step(ts(turns[:, :, :, :], turns[:, :, :, :], ROUND, None, ALU.subtract))
            fl = lambda a: a[:, :, :, :].rearrange("p n k e -> p (n k e)")
            for c in (TWO_PI_HI, TWO_PI_MID, TWO_PI_LO):
                step(stt(fl(ang), fl(turns), -float(c), fl(ang), ALU.mult, ALU.add))
            step(ts(ang[:, :, 1, :], ang[:, :, 1, :], float(np.pi / 2), None, ALU.add))
            step(ts(ang[:, :, :, :], ang[:, :, :, :], PI_SAFE, -PI_SAFE, ALU.min, ALU.max))
            dve.sem_inc(s_an, 1)

            def masks(g):
                dve.wait_ge(s_dist, B4 * (g + 1))
                ts(mask[:, B4 * g:B4 * g + B4, :], dist(g), (WINDOW / 2) ** 2, -BIG, ALU.is_ge, ALU.mult).then_inc(s_mask, 1)

            masks(0)
            masks(1)
            dve.wait_ge(s_wt, 2)
            cp(AT[:, :, :], bank[1][:, 0:D].rearrange("p (c o) -> p c o", c=KC)).then_inc(s_wtD, 1)
            cp(BT[:, :], bank[1][:, D:2 * D]).then_inc(s_wtD, 1)
            dve.wait_ge(s_wt, 4)
            for kc in range(KC):
                cp(WqT[:, kc, :, :].rearrange("p s (g d) -> p s g d", g=G),
                   bank[3][:, kc * D:(kc + 1) * D].rearrange("p (g s d) -> p s g d", g=G, s=GS)).then_inc(s_wtD, 1)

            for h in range(2):
                n4 = slice(4 * h, 4 * h + 4)
                dve.wait_ge(s_mixw, 16 * NT)
                for t in range(4 * h, 4 * h + 4):
                    tt(mix[:, t, :].rearrange("p (q d) -> p q d", q=B4),
                       mixw[:, t, :].unsqueeze(1).broadcast_to([P, B4, T]),
                       C("quad").unsqueeze(2).broadcast_to([P, B4, T]), ALU.mult).then_inc(s_ix, 1)
                ix[0] += 4
                dve.wait_ge(s_ix, ix[0])
                tt(mix[:, n4, :], mix[:, n4, :], ident.unsqueeze(1).broadcast_to([P, 4, P]), ALU.add).then_inc(s_mix, 1)

            dve.wait_ge(s_tab, 64)
            for u in range(4):
                n = UNITS[u][1] * WB if u < 3 else NWI
                cp(tab[0:n, u:u + 1], tab_i[0:n, u:u + 1]).then_inc(s_ix, 1)
            ix[0] += 4
            dve.wait_ge(s_ix, ix[0])
            for u in range(4):
                n = UNITS[u][1] * WB if u < 3 else NWI
                ts(diag[0:n, u, 0:n], C("ident", n, 0, n), tab[0:n, u:u + 1], None, ALU.mult).then_inc(s_diag, 1)
            step(tt(sel[0:NWI, 0, 0:B], slot[0:NWI, 3, 0:B], C("wr_seq", NWI), ALU.mult))
            step(dve.tensor_reduce(pick[0:NWI, 4:5], sel[0:NWI, 0, 0:B], AX.X, ALU.add))
            step(ts(wr[0:NWI, 0, :], C("wr_off", NWI), pick[0:NWI, 4:5], None, ALU.subtract))
            step(ts(wr[0:NWI, 1, :], wr[0:NWI, 0, :], 0.0, None, ALU.is_ge))
            step(stt(wr[0:NWI, 2, :], wr[0:NWI, 0, :], float(T - 1), wr[0:NWI, 1, :], ALU.is_le, ALU.mult))
            step(ts(wr[0:NWI, 0, :], wr[0:NWI, 0, :], C("wr_new", NWI), None, ALU.add))
            dve.wait_ge(s_brd, 1)
            stt(later[0:NWI, :], bank[7][0:NWI, B * WB:B * WB + NWI], tab[0:NWI, 3:4], C("later", NWI),
                ALU.is_equal, ALU.mult).then_inc(s_inr, 1)
            ts(hit[0:NWI, :], bank[7][0:NWI, 0:B * WB], tab[0:NWI, 3:4], None, ALU.is_equal).then_inc(s_inr, 1)
            dve.wait_ge(s_cnt, 1)
            step(stt(wr[0:NWI, 1, :], bank[7][0:NWI, 448:448 + BLOCK], 0.0, wr[0:NWI, 2, :], ALU.is_equal, ALU.mult))
            tt(wr[0:NWI, 3, :], wr[0:NWI, 1, :], wr[0:NWI, 0, :], ALU.mult).then_inc(s_val, 1)
            step(tt(sel[0:B, 1, 0:B], slot[0:B, 1, 0:B], C("ident", B, 0, B), ALU.mult))
            step(dve.tensor_reduce(pick[0:B, 5:6], sel[0:B, 1, 0:B], AX.X, ALU.add))
            step(cp(bits_i[0:B, 0:1], pick[0:B, 5:6]))
            for k in (1, 2, 3):
                ts(bits_i[0:B, k:k + 1], bits_i[0:B, 0:1], 1 << k, None, ALU.bitwise_and).then_inc(s_ix, 1)
            ix[0] += 3
            dve.wait_ge(s_ix, ix[0])
            step(ts(bits_i[0:B, 0:1], bits_i[0:B, 0:1], 1, None, ALU.bitwise_and))
            step(cp(bits[0:B, :], bits_i[0:B, :]))
            for k in (1, 2, 3):
                ts(bits[0:B, k:k + 1], bits[0:B, k:k + 1], 1.0 / (1 << k), None, ALU.mult).then_inc(s_ix, 1)
            ix[0] += 3
            dve.wait_ge(s_ix, ix[0])
            dve.wait_ge(s_adp, 16)
            dve.wait_ge(s_scal, 16)
            step(cp(amask[:, :], adp_i[:, :]))
            ts(amask[:, :], amask[:, :], C("adapter"), scal[:, 0:1], ALU.is_equal, ALU.mult).then_inc(s_am, 1)

            for h in range(2):
                dve.wait_ge(s_l0, 2 * h + 2)
                cp(x1T[:, 1, 512 * h:512 * h + 512], bank[(6, 1)[h]][:, :]).then_inc(s_x1D, 1)
            dve.wait_ge(s_am, 1)
            for h in range(2):
                dve.wait_ge(s_xa, h + 1)
                tt(xaT[:, 512 * h:512 * h + 512].rearrange("p (b t) -> p b t", t=T),
                   bank[2 + h][:, :].rearrange("p (b t) -> p b t", t=T),
                   amask[:, 16 * h:16 * h + 16].unsqueeze(2).broadcast_to([P, 16, T]), ALU.mult).then_inc(s_xas, 1)

            def permute(i):
                n = UNITS[LOADS[i][0]][1] * WB
                dve.wait_ge(s_bl[i % 3], 16 * (i // 3 + 1))
                if i >= 2:
                    dve.wait_ge(s_winw[i % 2], 16 * (i // 2))
                cp(blkp[0:n, i % 2, :].rearrange("p (o g d) -> p g o d", o=BLOCK, g=G),
                   blk[0:n, i % 3, :].rearrange("p (g o d) -> p g o d", g=G, o=BLOCK)).then_inc(s_perm, 1)

            dve.wait_ge(s_nrow, 1)
            step(stt(rows[:, 0, :], bank[7][0:B, 0:WROWS], 0.0, C("win_row", B), ALU.is_equal, ALU.mult))
            step(tt(rows[:, 1, :], rows[:, 0, :], bank[7][0:B, 0:WROWS], ALU.add))
            a, w = 1, WROWS
            for k in (3, 2, 1, 0):
                w -= 1 << k
                step(tt(rows[:, 2, 0:w], rows[:, a, (1 << k):(1 << k) + w], rows[:, a, 0:w], ALU.subtract))
                step(stt(rows[:, 1 - a, 0:w], rows[:, 2, 0:w], bits[0:B, k:k + 1], rows[:, a, 0:w], ALU.mult, ALU.add))
                a = 1 - a
            assert a == 1
            dve.sem_inc(s_rowf, 1)

            permute(0)
            permute(2)
            for k in range(4):
                oc, h = k % 2, k // 2
                dve.wait_ge(s_l1, k + 1)
                if k == 0:
                    dve.wait_ge(s_x1A, 2)
                    dve.wait_ge(s_x1D, 2)
                tt(x2T[:, oc, 512 * h:512 * h + 512], bank[(4, 5, 6, 0)[k]][:, :],
                   x1T[:, oc, 512 * h:512 * h + 512], ALU.add).then_inc(s_x2, 1)
            dve.wait_ge(s_rowT, 1)
            ts(rowA[:, :], bank[7][:, 200:200 + B], 1.0, None, ALU.subtract).then_inc(s_rowi, 1)
            for q in range(B4):
                ts(rowB[T * q:T * q + T, :], bank[7][0:KB, 240:240 + B].rearrange("p (n b) -> p n b", b=B4)[:, :, q],
                   1.0, None, ALU.subtract).then_inc(s_rowi, 1)
            permute(4)

            dve.wait_ge(s_norms, 32)
            step(ts(ns[:, :, 0, :], ns[:, :, 0, :], 1.0, None, ALU.add))
            step(cp(ns[:, :, 1, :], ns[:, :, 0, :]))
            step(ts(ns[:, :, 1, HD // 2:HD], ns[:, :, 1, HD // 2:HD], -1.0, None, ALU.mult))
            dve.wait_ge(s_tr, 1)
            for j in range(2):
                for k in range(2):
                    for hf in range(2):
                        e = slice(HD // 2 * hf, HD // 2 * hf + HD // 2)
                        tt(rot[:, j, k, :, e], trig[:, :, 1 - k, :],
                           ns[:, j, k, e].unsqueeze(1).broadcast_to([P, NT, HD // 2]), ALU.mult).then_inc(s_rt, 1)
            dve.wait_ge(s_rt, 8)

            nstep = [0]

            def nlink(ins):
                nstep[0] += 1
                ins.then_inc(s_nstep, 1)
                dve.wait_ge(s_nstep, nstep[0])

            def norm_rotate(xn, nh, ss, rr, j, t, roots, kept, kept_n, done):
                w = nh * HD
                heads = lambda a: a.rearrange("p (n h e) -> p n h e", n=2, e=HD)
                flat = lambda a: a[:, 0, 0:2 * w] if w == 128 else a[:, :, :].rearrange("p a b -> p (a b)")[:, 0:2 * w]
                sq, m2 = heads(flat(tmp)), heads(flat(tmp2))
                v = xn[:, 2 * t:2 * t + 2, 0:w]
                vh = v.rearrange("p n (h e) -> p n h e", e=HD)
                dve.wait_ge(kept, kept_n)
                nlink(tt(sq.rearrange("p n h e -> p n (h e)"), v, v, ALU.mult))
                dve.tensor_reduce(ss[:, 2 * t:2 * t + 2, :], sq, AX.X, ALU.add).then_inc(s_ss, 1)
                dve.wait_ge(s_rt2, roots)
                nlink(dve.reciprocal(rr[:, 2 * t:2 * t + 2, :], rr[:, 2 * t:2 * t + 2, :]))
                for n in range(2):
                    tt(vh[:, n], vh[:, n], rr[:, 2 * t + n, :].unsqueeze(2).broadcast_to([P, nh, HD]), ALU.mult) \
                        .then_inc(s_nstep, 1)
                nstep[0] += 2
                dve.wait_ge(s_nstep, nstep[0])
                for n in range(2):
                    tab_ = lambda k: rot[:, j, k, 2 * t + n, :].unsqueeze(1).broadcast_to([P, nh, HD])
                    tt(m2[:, n], vh[:, n], tab_(1), ALU.mult).then_inc(s_nstep, 1)
                    tt(sq[:, n], vh[:, n], tab_(0), ALU.mult).then_inc(s_nstep, 1)
                nstep[0] += 4
                dve.wait_ge(s_nstep, nstep[0])
                e0, e1 = slice(0, HD // 2), slice(HD // 2, HD)
                for n in range(2):
                    tt(vh[:, n, :, e0], sq[:, n, :, e0], m2[:, n, :, e1], ALU.add).then_inc(s_nstep, 1)
                    tt(vh[:, n, :, e1], sq[:, n, :, e1], m2[:, n, :, e0], ALU.add).then_inc(s_nstep, 1)
                nstep[0] += 4
                dve.wait_ge(s_nstep, nstep[0])
                dve.sem_inc(done, 1)

            for t in range(NT // 2):
                norm_rotate(kvn, G, ssk, rstdk, 1, t, t + 1, s_kvk, t + 1, s_kready)

            for g in range(2, NT):
                masks(g)
            for t in range(NT // 2):
                norm_rotate(qn, H, ssq, rstd, 0, t, NT // 2 + t + 1, s_qk, t + 1, s_qready)

            def keep_k(g):
                dve.wait_ge(s_kt, 2 * g + 1)
                if g >= 2:
                    dve.wait_ge(s_sc, B4 * (g - 1))
                cp(KT[:, g % 2, :, 0:P], bank[1][:, :].rearrange("p (b r) -> p b r", b=B4)).then_inc(s_kta, 1)

            def spread_v(g):
                dve.wait_ge(s_kvB[g % 3], 16 * (g // 3 + 1))
                if g == 0:
                    dve.wait_ge(s_vz, 1)
                if g >= 2:
                    dve.wait_ge(s_pv, B4 * (g - 1))
                for j in range(B4):
                    R = slice(KB * j, KB * j + KB)
                    cp(VBD[R, g % 2, j, :], kvB[R, g % 3, KV:2 * KV]).then_inc(s_vbd, 1)

            keep_k(0)
            spread_v(0)
            dve.wait_ge(s_mask, NT)

            def normalise(n):
                dve.wait_ge(s_exp, 2 * n + 2)
                dve.reciprocal(ri[:, n % 8, :], rs[:, n % 8, :]).then_inc(s_ri, 1)
                dve.wait_ge(s_ri, n + 1)
                e_ = pr[:, n // B4 % 2, :, n % B4, :]
                for u in range(2):
                    ts(e_[:, u, 0:P], e_[:, u, 0:P], ri[:, n % 8, u:u + 1], None, ALU.mult).then_inc(s_pn, 1)
                tt(prB[:, n // B4 % 2, :, n % B4, :], e_[:, :, P:KEYS],
                   ri[:, n % 8, :].unsqueeze(2).broadcast_to([P, 2, KB]), ALU.mult).then_inc(s_pn, 1)

            for n in range(B + 2 * B4 + 2):
                if n < B:
                    dve.wait_ge(s_sc, n + 1)
                    if n >= 2:
                        dve.wait_ge(s_exp, 2 * n - 2)
                    for u in range(2):
                        dve.tensor_tensor_reduce(S[:, n % 2, u, :], bank[3 + n % 2][:, u * KEYS:(u + 1) * KEYS], mask[:, n, :],
                                                 1.0, -3e38, ALU.add, ALU.max, mx[:, n % 4, u:u + 1]).then_inc(s_mx, 1)
                    dve.wait_ge(s_mx, 2 * n + 2)
                    ts(nb[:, n % 4, :], mx[:, n % 4, :], -SCALE, None, ALU.mult).then_inc(s_nb, 1)
                if 1 <= n <= B:
                    normalise(n - 1)
                if n % B4 == 2 and n // B4 + 1 < NT:
                    keep_k(n // B4 + 1)
                if n % B4 == 0 and 0 < n < B:
                    spread_v(n // B4)
                k = n - 6
                if k >= 0 and k % B4 == B4 - 1 and k < B:
                    g = k // B4
                    dve.wait_ge(s_pv, k + 1)
                    if g >= 2:
                        dve.wait_ge(s_wo, g - 1)
                    cp(oT[:, g % 2, :, :, :].rearrange("p b s t -> p b (s t)"),
                       bank[0][:, 0:D].rearrange("p (b c) -> p b c", b=B4)).then_inc(s_ot, 1)
                if k >= B4 and k % B4 == 0 and k // B4 <= NT:
                    g = k // B4 - 1
                    dve.wait_ge(s_wo, g + 1)
                    if g >= 2:
                        dve.wait_ge(s_l3, g - 1)
                    tt(x3T[:, g % 2, :, :], bank[7][:, 0:D].rearrange("p (c r) -> p c r", c=KC),
                       x2T[:, :, g * P:(g + 1) * P], ALU.add).then_inc(s_x3, 1)
                if k >= B4 and k % B4 == 1 and k // B4 <= NT:
                    g = k // B4 - 1
                    dve.wait_ge(s_l3, g + 1)
                    dve.wait_ge(s_be[g % 2], 16 * B4 * (g // 2 + 1))
                    if g >= 2:
                        dve.wait_ge(s_out[g % 2], 16 * (g // 2))
                    tt(res[:, g % 2, :], bank[7][:, D:2 * D], be[:, g % 2, :], ALU.add).then_inc(s_res, 1)

        @block.tensor
        def _(pe):
            mm, tr = pe.matmul, pe.transpose
            pe.wait_ge(s_cst, 16)

            def turn_square(j, src, m, waits):
                for s, v in waits:
                    pe.wait_ge(s, v)
                for kc in range(KC):
                    for oc in range(KC):
                        c0 = kc * D + oc * P
                        i_ = tr(bank[j][:, c0:c0 + P], src[:, oc, m, kc * P:(kc + 1) * P], ident)
                i_.then_inc(s_wt, 1)

            turn_square(0, nat, 0, [(s_w1, 16)])
            pe.wait_ge(s_ab, 48)
            for kc in range(KC):
                tr(bank[1][:, kc * P:(kc + 1) * P], natA[:, kc * P:(kc + 1) * P], ident)
            for oc in range(KC):
                i_ = tr(bank[1][:, D + oc * P:D + (oc + 1) * P], natB[:, oc, :], ident)
            i_.then_inc(s_wt, 1)
            turn_square(2, nat, 2, [(s_kvw, 32)])
            turn_square(3, nat, 1, [(s_qw, 16)])
            pe.wait_ge(s_wo_l, 16 * KC * GS)
            for s in range(GS):
                for oc in range(KC):
                    c0 = s * D + oc * P
                    i_ = tr(bank[4][:, c0:c0 + P],
                            nat[:, oc, 3, s * KV:(s + 1) * KV], ident)
            i_.then_inc(s_wt, 1)

            for h in range(2):
                pe.wait_ge(s_mix, h + 1)
                pe.wait_ge(s_x, 16 * (h + 1)) if h == 0 else pe.wait_ge(s_x, 32)
                if h == 0:
                    pe.wait_ge(s_x, 32)
                for c in range(KC):
                    if h == 1:
                        pe.wait_ge(*((s_wtA, 1), (s_wtD, 2))[c])
                    for t in range(4):
                        i_ = mm(bank[(5, 6, 0, 1)[2 * h + c]][:, t * P:(t + 1) * P], xin[:, 4 * h + t, c * P:(c + 1) * P],
                                mix[:, 4 * h + t, :], start=True, stop=True)
                    i_.then_inc(s_l0, 1)

            pe.wait_ge(s_diag, 4)
            pe.wait_ge(s_set, 3)
            for u in range(4):
                n = UNITS[u][1] * WB if u < 3 else NWI
                c0 = UNITS[u][0] * WB if u < 3 else B * WB
                i_ = mm(bank[7][0:NWI, c0:c0 + n], ones[0:n, 0:NWI], diag[0:n, u, 0:n], start=True, stop=True)
            i_.then_inc(s_brd, 1)
            pe.wait_ge(s_inr, 2)
            mm(bank[7][0:NWI, 448:448 + BLOCK], later[0:NWI, :], wr[0:NWI, 2, :], start=True, stop=True).then_inc(s_cnt, 1)

            pe.wait_ge(s_wtD, 4)
            pe.wait_ge(s_wtA, 3)
            for h in range(2):
                pe.wait_ge(s_x1A, h + 1)
                pe.wait_ge(s_x1D, h + 1)
                for kc in range(KC):
                    i_ = mm(bank[2 + h][:, :], AT[:, kc, :], x1T[:, kc, 512 * h:512 * h + 512], start=(kc == 0), stop=(kc == KC - 1))
                i_.then_inc(s_xa, 1)
            pe.wait_ge(s_val, 1)
            hits = hit[0:NWI, :].rearrange("p (b j) -> p b j", j=WB)
            for j in range(WB):
                i_ = mm(bank[7][0:B, j * BLOCK:(j + 1) * BLOCK], hits[:, :, j], wr[0:NWI, 3, :], start=True, stop=True)
            i_.then_inc(s_nrow, 1)
            for k in range(4):
                oc, h = k % 2, k // 2
                o = bank[(4, 5, 6, 0)[k]]
                for kc in range(KC):
                    mm(o[:, :], W1T[:, kc, oc * P:(oc + 1) * P], x1T[:, kc, 512 * h:512 * h + 512], start=(kc == 0), stop=False)
                pe.wait_ge(s_xas, h + 1)
                mm(o[:, :], BT[:, oc * P:(oc + 1) * P], xaT[:, 512 * h:512 * h + 512], start=False, stop=True).then_inc(s_l1, 1)
            pe.wait_ge(s_rowf, 1)
            tr(bank[7][:, 200:200 + B], rows[:, 1, 0:P], ident[0:B, 0:B])
            tr(bank[7][0:KB, 240:240 + B], rows[:, 1, P:KEYS], ident[0:B, 0:B]).then_inc(s_rowT, 1)

            for t in range(NT):
                if t % 4 == 0:
                    pe.wait_ge(s_x2, 2 * (t // 4 + 1))
                if t == 0:
                    pe.wait_ge(s_xas, 2)
                for kc in range(KC):
                    i_ = mm(bank[1 + t // 2][:, (t % 2) * D:(t % 2) * D + D], x2T[:, kc, t * P:(t + 1) * P], WkvT[:, kc, :],
                            start=(kc == 0), stop=(kc == KC - 1))
                if t % 2:
                    i_.then_inc(s_kvp, 1)
            for t in range(NT):
                if t == 6:
                    pe.wait_ge(s_rowi, 5)
                for kc in range(KC):
                    i_ = mm(bank[(5, 6, 0, 7)[t // 2]][:, (t % 2) * D:(t % 2) * D + D], x2T[:, kc, t * P:(t + 1) * P],
                            WqT[:, kc, :, :].rearrange("p s c -> p (s c)"), start=(kc == 0), stop=(kc == KC - 1))
                if t % 2:
                    i_.then_inc(s_qp, 1)

            def turn_k(g):
                if g >= 1:
                    pe.wait_ge(s_kta, g)
                else:
                    pe.wait_ge(s_kvk, NT // 2)
                for j in range(B4):
                    b = B4 * g + j
                    pe.wait_ge(s_kvA[b % NA], 16 * (b // NA + 1))
                    i_ = tr(bank[1][:, j * P:(j + 1) * P], kvA[:, b % NA, 0:KV], ident)
                i_.then_inc(s_kt, 1)
                if g >= 1:
                    pe.wait_ge(s_qt, G * g)
                pe.wait_ge(s_kvB[g % 3], 16 * (g // 3 + 1))
                tr(bank[2][:, 0:P], kvB[:, g % 3, 0:KV], ident)
                pe.wait_ge(s_qready, g // 2 + 1)
                for s in range(GS):
                    i_ = tr(bank[2][:, P + s * P:P + (s + 1) * P], qn[:, g, s * KV:(s + 1) * KV], ident)
                i_.then_inc(s_kt, 1)

            def scores(n):
                g, j = divmod(n, B4)
                if j == 0:
                    pe.wait_ge(s_kta, g + 1)
                    pe.wait_ge(s_ktb, g + 1)
                    pe.wait_ge(s_qt, G * (g + 1))
                if n >= 2:
                    pe.wait_ge(s_mx, 2 * (n - 1))
                for u in range(2):
                    i_ = mm(bank[3 + n % 2][:, u * KEYS:(u + 1) * KEYS],
                            QBD[:, g % 2, j, 2 * u:2 * u + 2, :].rearrange("p g c -> p (g c)"), KT[:, g % 2, j, :],
                            start=True, stop=True)
                i_.then_inc(s_sc, 1)

            def turn_probs(seq):
                g, j = divmod(seq, B4 + 1)
                pe.wait_ge(s_pn, 3 * (B4 * (g + 1) if j == 0 else B4 * g + j))
                if seq >= 2:
                    pe.wait_ge(s_pts, seq - 1)
                else:
                    pe.wait_ge(s_qk, 2)
                for u in range(2):
                    src = prB[:, g % 2, u, :, :].rearrange("p b r -> p (b r)") if j == 0 else pr[:, g % 2, u, j - 1, 0:P]
                    i_ = tr(bank[5 + seq % 2][:, u * P:(u + 1) * P], src, ident)
                i_.then_inc(s_pt, 1)

            def pv(n):
                g, j = divmod(n, B4)
                pe.wait_ge(s_pts, g * (B4 + 1) + j + 2)
                if j == 0:
                    if g:
                        pe.wait_ge(s_ot, g)
                    else:
                        pe.wait_ge(s_qk, 3)
                pe.wait_ge(s_vbd, B4 * (g + 1))
                for k in range(G):
                    o = bank[0][HD * k:HD * k + HD, j * GS * T:(j + 1) * GS * T]
                    c = slice(GS * T * (k % 2), GS * T * (k % 2) + GS * T)
                    v = slice(KV + HD * k, KV + HD * k + HD)
                    mm(o, kvA[:, n % NA, v], PTA[:, n % 3, k // 2, c], start=True, stop=False)
                    i_ = mm(o, VBD[:, g % 2, j, HD * k:HD * k + HD], PTB[:, g % 2, k // 2, c], start=False, stop=True)
                i_.then_inc(s_pv, 1)

            def project(g):
                pe.wait_ge(s_ot, g + 1)
                if g:
                    pe.wait_ge(s_res, g)
                else:
                    pe.wait_ge(s_qk, 4)
                for oc in range(KC):
                    for s in range(GS):
                        i_ = mm(bank[7][:, oc * P:(oc + 1) * P], WoT[:, s, oc * P:(oc + 1) * P], oT[:, g % 2, :, s, :],
                                start=(s == 0), stop=(s == GS - 1))
                i_.then_inc(s_wo, 1)

            def layer3(g):
                pe.wait_ge(s_x3, g + 1)
                o = bank[7][:, D:2 * D]
                for kc in range(KC):
                    mm(o[:, kc * P:(kc + 1) * P], x3T[:, g % 2, kc, :], ident, start=(kc == 0), stop=False, skip_group_check=True)
                for j in range(B4):
                    b = B4 * g + j
                    pe.wait_ge(s_we[b % NE], 16 * (b // NE + 1))
                    for kc in range(KC):
                        i_ = mm(o[T * j:T * j + T, :], x3T[:, g % 2, kc, T * j:T * j + T], We[:, b % NE, kc, :],
                                start=False, stop=(kc == KC - 1), skip_group_check=True)
                i_.then_inc(s_l3, 1)

            turn_k(0)
            for n in range(B + 2 * B4 + 2):
                if n < B:
                    scores(n)
                if n % B4 == 2 and n // B4 + 1 < NT:
                    turn_k(n // B4 + 1)
                m = n - B4
                if 0 <= m < B:
                    if m % B4 == 0:
                        turn_probs(m // B4 * (B4 + 1))
                    turn_probs(m // B4 * (B4 + 1) + m % B4 + 1)
                k = n - 5
                if 0 <= k < B:
                    pv(k)
                k = n - 6
                if k >= 0 and k % B4 == B4 - 1 and k < B:
                    project(k // B4)
                if k >= B4 and k % B4 == 0 and k // B4 <= NT:
                    layer3(k // B4 - 1)


_INS = ["x", "itok_B_1_198", "itok_B_0_6", "itok_Bx257_0_4111", "itok_B_37_3939", "itok_B_0_15", "L0_cond_weights",
        "L1_cond_W", "L1_cond_A", "L1_cond_Bm", "L1_cond_scalings", "L2_cond_Wq", "L2_cond_Wk", "L2_cond_Wv",
        "L2_cond_Wo", "L2_cond_q_norm_scale", "L2_cond_k_norm_scale", "L2_cond_k_blocks", "L2_cond_v_blocks",
        "L3_cond_W", "L3_cond_b"]


def kernel(**inputs):
    from concourse import bacc
    from concourse.bass_utils import run_bass_kernel_spmd

    nc = bacc.Bacc("TRN2", target_bir_lowering=False, num_devices=1)
    arrays, args = {}, []
    for name in _INS:
        a = np.ascontiguousarray(inputs[name])
        arrays[f"in_{name}"] = a
        args.append(nc.dram_tensor(f"in_{name}", a.shape, mybir.dt.from_np(a.dtype), kind="ExternalInput").ap())
    c = Columns().data
    arrays["in_consts"] = c
    args.append(nc.dram_tensor("in_consts", c.shape, F32, kind="ExternalInput").ap())
    args.append(nc.dram_tensor("out", (B, T, D), F32, kind="ExternalOutput").ap())
    program(nc, *args)
    r = run_bass_kernel_spmd(nc, [arrays], core_ids=[0])
    return r.results[0]["out"]
```

```python
from contextlib import ExitStack

import numpy as np

import concourse.bass as bass
from concourse import mybir
from concourse.alu_op_type import AluOpType as ALU

ACT = mybir.ActivationFunctionType
AX = mybir.AxisListType
F32 = mybir.dt.float32
BF16 = mybir.dt.bfloat16
I32 = mybir.dt.int32

P = 128
B, T, D = 32, 32, 256
KC = D // P
B4 = P // T
NT = B // B4
H, G, HD = 8, 4, 32
GS = H // G
KV = G * HD
BLOCK, WINDOW, NBLK = 16, 128, 257
SLOTS = 257
NPOOL = 16 * NBLK
SCALE = float(D) ** -0.5
EPS = 1e-6
THETA = 10000.0
ADAPTERS, RANK = 8, 16
EXPERTS = 16
NCOND = 200
KEYS = 160
KB = KEYS - P
WB = 11
WROWS = WB * BLOCK
SEQ_U = 11
UNITS = [(0, 11), (11, 11), (22, 10)]
NW = 3
NWI = B * NW
NEW0 = 0
WIN0 = NEW0 + B * T
NROWS = WIN0 + B * WROWS
BIG = 1e30
TURN, PV, TAIL = 6, 7, 12
AHEAD = 8
TWO_PI_HI = 6.28125
TWO_PI_MID = 0.0019350051879882812
TWO_PI_LO = 2 * np.pi - TWO_PI_HI - TWO_PI_MID
ROUND = 12582912.0
PI_SAFE = 3.1415925


EARLY = ("unit_seq", "unit_blk", "unit_row", "wr_seq", "wr_blk", "wr_row", "in_tile", "quad", "inv")
LATE = ("ident",)


class Columns:

    def __init__(self):
        p = np.arange(P)
        r = lambda a: np.broadcast_to(np.asarray(a, np.float32), (P, len(a)))
        c = lambda a: np.asarray(a, np.float32).reshape(P, -1)
        half = HD // 2
        inv = (np.float32(1.0) / np.power(np.float32(THETA), np.arange(half, dtype=np.float32) / np.float32(half)))
        parts = {
            "ident": np.eye(P),
            "iota": r(np.arange(KEYS)),
            "inv": r(inv.astype(np.float32)),
            "quad": c([[q // T == j for j in range(B4)] for q in p]),
            "in_tile": c(p % T),
            "unit_seq": c([[q // WB == j for j in range(SEQ_U)] for q in p]),
            "unit_blk": c(p % WB),
            "unit_row": c([[min(u * SEQ_U + q // WB, B - 1) * SLOTS for u in range(3)] for q in p]),
            "wr_seq": c([[q // NW == j for j in range(B)] for q in p]),
            "wr_blk": c(p % NW),
            "wr_row": c(np.minimum(p // NW, B - 1) * SLOTS),
            "wr_off": c([[BLOCK * (q % NW) + o for o in range(BLOCK)] for q in p]),
            "wr_new": c(p // NW * T + NEW0 + 1),
            "later": c([[i < q for i in range(NWI)] for q in p]),
            "win_row": c([[WIN0 + q * WROWS + x + 1 for x in range(WROWS)] for q in p]),
            "adapter": c(p // RANK),
        }
        self.at, self.data, n = {}, [], 0
        parts = {**{k: parts[k] for k in EARLY}, **{k: v for k, v in parts.items() if k not in EARLY}}
        for k, v in parts.items():
            v = np.asarray(v, np.float32)
            if k == LATE[0]:
                self.early = n
            self.at[k] = (n, n + v.shape[1])
            self.data.append(v)
            n += v.shape[1]
        self.width = n
        self.data = np.ascontiguousarray(np.concatenate(self.data, 1), np.float32)


def program(nc, x, cond, adapter_idx, table, kv_lens, expert_ids, W0, W1, A1, B1, s1, Wq, Wk, Wv, Wo, q_norm, k_norm,
            k_blocks, v_blocks, W3, b3, consts, out):
    cols = Columns()
    ctx = ExitStack()

    def sb(name, shape, dt=F32):
        return ctx.enter_context(nc.sbuf_tensor(name, shape, dt))

    def sem(name):
        return ctx.enter_context(nc.semaphore(name))

    with ctx:
        mix_rows = nc.dram_tensor("mix_rows", [B * T, T], F32).ap()
        kv_rows = nc.dram_tensor("kv_rows", [NROWS, 2 * KV], F32).ap()

        cst = sb("cst", [P, cols.width])

        def C(name, parts=P, a=0, b=None):
            lo, hi = cols.at[name]
            return cst[0:parts, lo + a:(hi if b is None else lo + b)]

        ident = C("ident")
        ones = sb("ones", [P, P])
        nat = sb("nat", [P, 2, 4, D])
        natA = sb("natA", [P, D])
        natB = sb("natB", [P, KC, P])
        W1T = sb("W1T", [P, KC, D])
        WkvT = sb("WkvT", [P, KC, 2 * KV])
        WqT = sb("WqT", [P, KC, GS, KV])
        WoT = sb("WoT", [P, GS, D])
        AT = sb("AT", [P, KC, P])
        BT = sb("BT", [P, D])
        xin = sb("xin", [P, NT, D])
        mixw = sb("mixw", [P, NT, T])
        kvn = sb("kvn", [P, NT, 2 * KV])
        mixg = kvn[0:B, 0:4, :].rearrange("p n c -> p (n c)")
        mix = sb("mix", [P, NT, P])
        x1T = sb("x1T", [P, KC, B * T])
        qn = x1T[:, :, :].rearrange("p c r -> p (c r)").rearrange("p (n c) -> p n c", n=NT)
        x2T = sb("x2T", [P, KC, B * T])
        xaT = sb("xaT", [P, B * T])

        ksq = sb("ksq", [P, NT, KV])
        ksn = sb("ksn", [P, NT, KV])
        ssq = sb("ssq", [P, NT, H])
        rstd = sb("rstd", [P, NT, H])
        ssk = sb("ssk", [P, NT, G])
        rstdk = sb("rstdk", [P, NT, G])
        eps = sb("eps", [P, 1])
        blk = sb("blk", [P, 3, BLOCK * KV])
        qsq, qcs, qsn = (blk[:, i, :].rearrange("p (n c) -> p n c", n=NT) for i in range(3))
        blkp = sb("blkp", [P, 2, BLOCK * KV])
        lens_i = sb("lens_i", [P, B + 1], I32)
        cond_i = sb("cond_i", [B, 1], I32)
        adp_i = sb("adp_i", [P, B], I32)
        ids_i = sb("ids_i", [1, B], I32)
        lens = sb("lens", [P, B + 1])
        first = sb("first", [P, B + 1])
        first_i = sb("first_i", [P, B + 1], I32)
        slot_i = sb("slot_i", [P, 4, B + 1], I32)
        slot = sb("slot", [P, 4, B + 1])
        sel = sb("sel", [P, 4, B + 1])
        pick = sb("pick", [P, 8])
        tidx = sb("tidx", [P, 4])
        tidx_i = sb("tidx_i", [P, 4], I32)
        tab_i = sb("tab_i", [P, 4], I32)
        tab = sb("tab", [P, 4])
        diag = sb("diag", [P, 4, P])
        hit = sb("hit", [P, B * WB])
        later = sb("later", [P, NWI])
        wr = sb("wr", [P, 4, BLOCK])
        bits_i = sb("bits_i", [P, 4], I32)
        bits = sb("bits", [P, 4])
        rows = sb("rows", [B, 3, WROWS])
        rowA = sb("rowA", [P, B], I32)
        rowB = sb("rowB", [P, NT], I32)
        scal = sb("scal", [P, 1])
        amask = sb("amask", [P, B])
        pos = sb("pos", [P, NT])
        ang = sb("ang", [P, NT, 2, HD // 2])
        turns = sb("turns", [P, NT, 2, HD // 2])
        trig = sb("trig", [P, NT, 2, HD // 2])
        ns = sb("ns", [P, 2, 2, HD])
        rot = sb("rot", [P, 2, 2, NT, HD])
        hi = sb("hi", [P, B])
        sel8 = sb("sel8", [P, NT, B4])
        mask = sb("mask", [P, B, KEYS], BF16)
        NA = 16
        kvA = sb("kvA", [P, NA, 2 * KV])
        kvB_own = sb("kvB", [P, NT // 2, 2 * KV])
        VBD = xin[:, 0:4, :].rearrange("p n c -> p (n c)").rearrange("p (g b c) -> p g b c", g=2, b=B4)
        kvB = lambda g, c: kvB_own[:, g, c] if g < NT // 2 else xin[:, g, c]
        KT = sb("KT", [P, 2, B4, KEYS])
        QBD = sb("QBD", [P, 2, B4, G, GS * T])
        S = sb("S", [P, 2, 2, KEYS])
        pr = sb("pr", [P, 2, 2, B4, KEYS])
        prB = sb("prB", [P, 2, 2, B4, KB])
        nb = sb("nb", [P, 4, 2])
        rs = sb("rs", [P, 8, 2])
        ri = sb("ri", [P, 8, 2])
        PTA = sb("PTA", [P, 3, 2, P])
        PTB = sb("PTB", [P, 2, 2, P])
        oT = sb("oT", [P, 2, B4, GS, T])
        x3T = sb("x3T", [P, 2, KC, P])
        NE = 4
        We = sb("We", [P, NE, KC, D])
        be = sb("be", [P, 2, D])
        res = nat[:, :, 0, :]
        bank = [ctx.enter_context(nc.psum_tensor(f"bank{i}", [P, 512], F32)) for i in range(8)]

        s_cst0 = sem("cst_early_loaded")
        s_cst, s_lens, s_cond, s_adp, s_ids, s_x = (sem(f"{n}_loaded") for n in ("cst", "lens", "cond", "adp", "ids", "x"))
        s_scal, s_norms, s_wo_l = sem("scal_loaded"), sem("norms_loaded"), sem("wo_loaded")
        s_w1, s_ab, s_kvw, s_qw = sem("w1_loaded"), sem("ab_loaded"), sem("kvw_loaded"), sem("qw_loaded")
        s_set = sem("constants_set")
        s_ix = sem("index_step")
        s_tidx, s_tab = sem("table_index_ready"), sem("table_read")
        s_mixg, s_mixs, s_mixw = sem("mix_gathered"), sem("mix_in_scratch"), sem("mix_loaded")
        s_kn, s_ksin, s_qn, s_qsin, s_pb = (sem(n) for n in ("k_scaled", "k_sines_ready", "q_scaled", "q_sines_ready", "tail_probs_ready"))
        s_bl = [sem(f"blocks_loaded{i}") for i in range(3)]
        s_perm = sem("blocks_permuted")
        s_winw = [sem(f"window_written{i}") for i in range(2)]
        s_neww = sem("new_rows_written")
        s_diag, s_brd, s_inr, s_cnt, s_val, s_nrow, s_rowf, s_rowT, s_rowi = (
            sem(n) for n in ("diagonals_ready", "blocks_broadcast", "writers_ready", "overwrites_counted", "valid_ready",
                             "new_row_found", "key_rows_ready", "key_rows_turned", "key_rows_int"))
        s_wt, s_wtA, s_wtD = sem("weights_turned"), sem("weights_kept_act"), sem("weights_kept_dve")
        s_mix = sem("mix_ready")
        s_l0, s_x1A, s_x1D = sem("mix_done"), sem("x1_kept_act"), sem("x1_kept_dve")
        s_xa, s_xas, s_l1, s_x2 = sem("down_done"), sem("down_kept"), sem("layer1_done"), sem("x2_kept")
        s_am = sem("adapter_mask_ready")
        s_kvp, s_kvk, s_qp, s_qk = sem("kv_projected"), sem("kv_kept"), sem("q_projected"), sem("q_kept")
        s_an, s_tr, s_rt = sem("angles_ready"), sem("trig_ready"), sem("rotation_ready")
        s_sqr, s_ss, s_rt2, s_nstep, s_rot2, s_kready, s_qready = (
            sem(n) for n in ("squares_ready", "sums_ready", "roots_ready", "norm_step", "rotated_half", "k_ready", "q_ready"))
        s_hi, s_dist, s_mask = sem("middles_ready"), sem("distances_ready"), sem("masks_ready")
        dist = lambda g: pr[:, g % 2, g // 2 % 2, :, :]
        s_kvA = [sem(f"kvA_loaded{i}") for i in range(NA)]
        s_kvB = [sem(f"kvB_loaded{i}") for i in range(NT)]
        s_kt, s_kta, s_ktb, s_qt = sem("k_turned"), sem("kA_kept"), sem("kB_kept"), sem("q_kept_diagonal")
        s_qz, s_vbd = sem("q_diagonal_zeroed"), sem("v_diagonal_ready")
        s_sc, s_mx, s_nb, s_exp, s_ri, s_pn = (sem(n) for n in (
            "scores_ready", "max_ready", "bias_ready", "exp_ready", "inverse_ready", "probs_ready"))
        s_pt, s_pts, s_pv, s_ot = sem("probs_turned"), sem("probs_kept"), sem("pv_done"), sem("o_kept")
        s_wo, s_x3, s_l3, s_res = sem("wo_done"), sem("x3_kept"), sem("layer3_done"), sem("result_ready")
        s_we = [sem(f"expert_loaded{i}") for i in range(NE)]
        s_be = [sem(f"expert_bias_loaded{i}") for i in range(2)]
        s_out = [sem(f"output_written{i}") for i in range(2)]

        k_heads = lambda h: kvn[:, 4 * h:4 * h + 4, 0:KV].rearrange("p n (h e) -> p n h e", e=HD)
        q_heads = lambda h: qn[:, 4 * h:4 * h + 4, :].rearrange("p n (h e) -> p n h e", e=HD)
        of_half = lambda t, h: t[:, 4 * h:4 * h + 4, :].rearrange("p n (h e) -> p n h e", e=HD)
        k_sq, k_sin = (lambda h: of_half(ksq, h)), (lambda h: of_half(ksn, h))
        q_sq, q_cos, q_sin = (lambda h: of_half(qsq, h)), (lambda h: of_half(qcs, h)), (lambda h: of_half(qsn, h))
        table_of = lambda j, k, h, nh: rot[:, j, k, 4 * h:4 * h + 4, :].unsqueeze(2).broadcast_to([P, 4, nh, HD])
        turned = lambda m: m // B4 * (B4 + 1) + m % B4 + 2

        block = ctx.enter_context(nc.Block())

        pool_k = k_blocks.rearrange("n g o d -> n (g o d)")
        pool_v = v_blocks.rearrange("n g o d -> n (g o d)")
        LOADS = [(u, kv) for u in range(3) for kv in range(2)]
        out_rows = out.rearrange("b t d -> (b t) d").rearrange("(n p) d -> n p d", p=P)

        @block.sync
        def _(sp):
            sp.dma_start(cond_i[:, :], cond.unsqueeze(1)).then_inc(s_cond, 16)
            sp.dma_start(lens_i[:, 0:B], kv_lens.partition_broadcast(P)).then_inc(s_lens, 16)
            sp.dma_start(cst[:, 0:cols.early], consts[:, 0:cols.early]).then_inc(s_cst0, 16)
            sp.dma_start(nat[:, :, 0, :], W1.rearrange("(c p) d -> p c d", p=P)).then_inc(s_w1, 16)
            for j in range(2):
                sp.dma_start(xin[:, 4 * j:4 * j + 4, :],
                             x.rearrange("b c t -> (b c) t").rearrange("(n p) t -> p n t", p=P)[:, 4 * j:4 * j + 4, :]) \
                    .then_inc(s_x, 16)
            sp.wait_ge(s_mixg, 16)
            sp.dma_start(mix_rows.rearrange("(b c) d -> b (c d)", c=T), mixg).then_inc(s_mixs, 16)
            sp.wait_ge(s_mixs, 16)
            sp.dma_start(mixw[:, :, :], mix_rows.rearrange("(n p) d -> p n d", p=P)).then_inc(s_mixw, 16)
            sp.dma_start(nat[:, 0, 2, :], Wk).then_inc(s_kvw, 16)
            sp.dma_start(nat[:, 1, 2, :], Wv).then_inc(s_kvw, 16)
            sp.dma_start(nat[:, :, 1, :], Wq.rearrange("(c p) d -> p c d", p=P)).then_inc(s_qw, 16)

            for i, (u, kv) in enumerate(LOADS):
                b0, nb_ = UNITS[u]
                n = nb_ * WB
                sp.wait_ge(s_perm, i + 1)
                r0 = WIN0 + b0 * WROWS
                dst = kv_rows[r0:r0 + n * BLOCK, kv * KV:(kv + 1) * KV].rearrange("(p o) c -> p o c", o=BLOCK)
                sp.dma_start(dst, blkp[0:n, i % 2, :].rearrange("p (o c) -> p o c", o=BLOCK)).then_inc(s_winw[i % 2], 16)
            for h in range(2):
                sp.wait_ge(s_kready, h + 1)
                r0 = NEW0 + 4 * h * P
                sp.dma_start(kv_rows[r0:r0 + 4 * P, :].rearrange("(j p) c -> p j c", p=P),
                             kvn[:, 4 * h:4 * h + 4, :]).then_inc(s_neww, 16)
            sp.wait_ge(s_ids, 16)

            def expert(b):
                g = b // B4
                if b >= NE:
                    sp.wait_ge(s_l3, (b - NE) // B4 + 1)
                if g >= 2 and b % B4 == 0:
                    sp.wait_ge(s_res, g - 1)
                e = sp.value_load(ids_i[0:1, b:b + 1], min_val=0, max_val=EXPERTS - 1)
                sp.dma_start(We[:, b % NE, :, :], W3[bass.ds(e, 1), :, :].rearrange("e (c p) o -> p (e c) o", p=P)) \
                    .then_inc(s_we[b % NE], 16)
                sp.dma_start(be[T * (b % B4):T * (b % B4) + T, g % 2, :],
                             b3[bass.ds(e, 1), :].rearrange("e o -> (e o)").partition_broadcast(T)).then_inc(s_be[g % 2], 16)

            for b in range(NE):
                expert(b)
            nxt = NE
            for g in range(NT):
                while nxt < B and (nxt - NE) // B4 <= g and not (nxt % B4 == 0 and nxt // B4 - 1 > g):
                    expert(nxt)
                    nxt += 1
                sp.wait_ge(s_res, g + 1)
                sp.dma_start(out_rows[g], res[:, g % 2, :]).then_inc(s_out[g % 2], 16)
            assert nxt == B
            for j in range(2):
                sp.wait_ge(s_out[j], 16 * NT // 2)

        @block.gpsimd
        def _(pool):
            pool.memset(ones[:, :], 1.0).then_inc(s_set, 1)
            pool.memset(lens_i[:, B:B + 1], 0).then_inc(s_set, 1)
            pool.memset(eps[:, :], EPS).then_inc(s_set, 1)
            for j in range(2):
                pool.memset(QBD[:, j, :, :, :], 0.0).then_inc(s_qz, 1)
            pool.wait_ge(s_cond, 16)
            pool.indirect_dma_start(out=mixg, out_offset=None, in_=W0.rearrange("s c d -> s (c d)"),
                                    in_offset=bass.IndirectOffsetOnAxis(ap=cond_i[:, :], axis=0)).then_inc(s_mixg, 16)
            pool.wait_ge(s_tidx, 1)
            table_1 = table.rearrange("b s -> (b s)").unsqueeze(1)
            for u in range(4):
                n = UNITS[u][1] * WB if u < 3 else NWI
                pool.indirect_dma_start(out=tab_i[0:n, u:u + 1], out_offset=None, in_=table_1,
                                        in_offset=bass.IndirectOffsetOnAxis(ap=tidx_i[0:n, u:u + 1], axis=0)).then_inc(s_tab, 16)
            pool.wait_ge(s_tab, 64)

            def load_blocks(i):
                u, kv = LOADS[i]
                n = UNITS[u][1] * WB
                if i >= 3:
                    pool.wait_ge(s_perm, i - 2)
                pool.indirect_dma_start(out=blk[0:n, i % 3, :], out_offset=None, in_=(pool_k, pool_v)[kv],
                                        in_offset=bass.IndirectOffsetOnAxis(ap=tab_i[0:n, u:u + 1], axis=0)).then_inc(s_bl[i % 3], 16)

            for i in range(3):
                load_blocks(i)
            for i in range(6):
                n = UNITS[LOADS[i][0]][1] * WB
                pool.wait_ge(s_bl[i % 3], 16 * (i // 3 + 1))
                if i >= 2:
                    pool.wait_ge(s_winw[i % 2], 16 * (i // 2))
                pool.tensor_copy(blkp[0:n, i % 2, :].rearrange("p (o g d) -> p g o d", o=BLOCK, g=G),
                                 blk[0:n, i % 3, :].rearrange("p (g o d) -> p g o d", g=G, o=BLOCK)).then_inc(s_perm, 1)
                if i + 3 < 6:
                    load_blocks(i + 3)
            for h in range(2):
                pool.wait_ge(s_kn, h + 1)
                pool.tensor_tensor(k_sin(h), k_heads(h), table_of(1, 1, h, G), ALU.mult).then_inc(s_ksin, 1)

            def gather_b(g):
                pool.indirect_dma_start(out=kvB(g, slice(0, 2 * KV)), out_offset=None, in_=kv_rows,
                                        in_offset=bass.IndirectOffsetOnAxis(ap=rowB[:, g:g + 1], axis=0)) \
                    .then_inc(s_kvB[g], 16)

            def gather_a(b):
                if b >= NA:
                    pool.wait_ge(s_pv, b - NA + 1)
                if b % B4 == 0:
                    gather_b(b // B4)
                pool.indirect_dma_start(out=kvA[:, b % NA, :], out_offset=None, in_=kv_rows,
                                        in_offset=bass.IndirectOffsetOnAxis(ap=rowA[:, b:b + 1], axis=0)).then_inc(s_kvA[b % NA], 16)

            pool.wait_ge(s_l0, 4)
            pool.wait_ge(s_rowi, 5)
            for j in range(2):
                pool.wait_ge(s_winw[j], 48)
            pool.wait_ge(s_neww, 32)
            for b in range(B4):
                gather_a(b)
            for h in range(2):
                pool.wait_ge(s_qn, h + 1)
                pool.tensor_tensor(q_sin(h), q_heads(h), table_of(0, 1, h, H), ALU.mult).then_inc(s_qsin, 1)
            for b in range(B4, AHEAD):
                gather_a(b)
            pool.wait_ge(s_cst0, 16)
            for n in range(B + 2):
                if n % B4 == 3 and n // B4 < NT:
                    g = n // B4
                    pool.wait_ge(s_kvB[g], 16)
                    if g >= 2:
                        pool.wait_ge(s_pv, B4 * (g - 1))
                    pool.tensor_tensor(VBD[:, g % 2, :, :],
                                       kvB(g, slice(KV, 2 * KV)).unsqueeze(1).broadcast_to([P, B4, KV]),
                                       C("quad").unsqueeze(2).broadcast_to([P, B4, KV]), ALU.mult).then_inc(s_vbd, 1)
                if n >= 2:
                    k = n - 2
                    pool.wait_ge(s_ri, k + 1)
                    pool.tensor_tensor(prB[:, k // B4 % 2, :, k % B4, :], pr[:, k // B4 % 2, :, k % B4, P:KEYS],
                                       ri[:, k % 8, :].unsqueeze(2).broadcast_to([P, 2, KB]), ALU.mult).then_inc(s_pb, 1)
                if n + AHEAD < B:
                    gather_a(n + AHEAD)

        @block.scalar
        def _(act):
            act.dma_start(cst[:, cols.early:], consts[:, cols.early:]).then_inc(s_cst, 16)
            act.dma_start(natA[:, :], A1.rearrange("n r d -> (n r) d")).then_inc(s_ab, 16)
            for oc in range(KC):
                act.dma_start(natB[:, oc, :].rearrange("p (n r) -> p n r", r=RANK),
                              B1[:, oc * P:(oc + 1) * P, :].rearrange("n o r -> o n r")).then_inc(s_ab, 16)
            act.dma_start(adp_i[:, :], adapter_idx.partition_broadcast(P)).then_inc(s_adp, 16)
            act.dma_start(scal[:, :], s1.unsqueeze(1).broadcast_to([ADAPTERS, RANK])).then_inc(s_scal, 16)
            for j, w in enumerate((q_norm, k_norm)):
                act.dma_start(ns[:, j, 0, :], w.partition_broadcast(P)).then_inc(s_norms, 16)
            act.dma_start(ids_i[:, :], expert_ids.unsqueeze(0)).then_inc(s_ids, 16)
            for oc in range(KC):
                for s in range(GS):
                    act.dma_start(nat[:, oc, 3, s * KV:(s + 1) * KV].rearrange("p (g d) -> p g d", g=G),
                                  Wo[oc * P:(oc + 1) * P, :].rearrange("p (g s d) -> p s g d", g=G, s=GS)[:, s]) \
                        .then_inc(s_wo_l, 16)

            for k, (src, dst) in enumerate(((0, W1T), (2, WkvT), (4, WoT))):
                act.wait_ge(s_wt, src + 1)
                act.copy(dst[:, :, :], bank[src][:, :].rearrange("p (c o) -> p c o", c=2)).then_inc(s_wtA, 1)
            def distances(g):
                if g == 0:
                    act.wait_ge(s_hi, 1)
                if g >= 4:
                    act.wait_ge(s_mask, g - 3)
                for j in range(B4):
                    act.activation(dist(g)[:, j, :], C("iota"), ACT.Square, bias=hi[:, B4 * g + j:B4 * g + j + 1]) \
                        .then_inc(s_dist, 1)

            act.wait_ge(s_cst, 16)
            for g in range(NT // 2):
                distances(g)
            act.wait_ge(s_an, 1)
            act.activation(trig[:, :, :, :], ang[:, :, :, :], ACT.Sin).then_inc(s_tr, 1)
            for h in range(2):
                act.wait_ge(s_l0, 2 * h + 1)
                act.copy(x1T[:, 0, 512 * h:512 * h + 512], bank[(5, 0)[h]][:, :]).then_inc(s_x1A, 1)

            for g in range(NT // 2, NT):
                distances(g)
            for t in range(NT // 2):
                act.wait_ge(s_kvp, t + 1)
                b_ = bank[1 + t][:, :].rearrange("p (j c) -> p j c", j=2)
                act.copy(kvn[:, 2 * t:2 * t + 2, :], b_).then_inc(s_kvk, 1)
                act.activation(ksq[:, 2 * t:2 * t + 2, :], b_[:, :, 0:KV], ACT.Square).then_inc(s_kvk, 1)
            for h in range(2):
                act.wait_ge(s_ss, h + 1)
                act.activation(rstdk[:, 4 * h:4 * h + 4, :], ssk[:, 4 * h:4 * h + 4, :], ACT.Sqrt,
                               bias=eps[:, 0:1], scale=1.0 / HD).then_inc(s_rt2, 1)
            act.wait_ge(s_perm, 6)
            for t in range(NT // 2):
                act.wait_ge(s_qp, t + 1)
                b_ = bank[(5, 6, 0, 7)[t]][:, :].rearrange("p (j c) -> p j c", j=2)
                act.copy(qn[:, 2 * t:2 * t + 2, :], b_).then_inc(s_qk, 1)
                act.activation(qsq[:, 2 * t:2 * t + 2, :], b_, ACT.Square).then_inc(s_qk, 1)
            for h in range(2):
                act.wait_ge(s_ss, h + 3)
                act.activation(rstd[:, 4 * h:4 * h + 4, :], ssq[:, 4 * h:4 * h + 4, :], ACT.Sqrt,
                               bias=eps[:, 0:1], scale=1.0 / HD).then_inc(s_rt2, 1)

            def keep_q(g):
                act.wait_ge(s_kt, 2 * g + 2)
                if g >= 2:
                    act.wait_ge(s_sc, B4 * (g - 1))
                act.copy(KT[:, g % 2, :, P:KEYS], bank[2][:, 0:P].rearrange("p (b r) -> p b r", b=B4)).then_inc(s_ktb, 1)
                if g == 0:
                    act.wait_ge(s_qz, 2)
                for k in range(G):
                    q = slice(HD * k, HD * k + HD)
                    act.copy(QBD[q, g % 2, :, k, :].rearrange("p b (s t) -> p s b t", s=GS),
                             bank[2][q, P:P + 2 * P].rearrange("p (s b t) -> p s b t", s=GS, b=B4)).then_inc(s_qt, 1)

            def keep_probs(seq):
                g, j = divmod(seq, B4 + 1)
                act.wait_ge(s_pt, seq + 1)
                if j == 0:
                    if g >= 2:
                        act.wait_ge(s_pv, B4 * (g - 1))
                    dst = PTB[:, g % 2, :, :]
                else:
                    m = B4 * g + j - 1
                    if m >= 3:
                        act.wait_ge(s_pv, m - 2)
                    dst = PTA[:, m % 3, :, :]
                act.copy(dst, bank[5 + seq % 2][:, 0:2 * P].rearrange("p (u r) -> p u r", u=2)).then_inc(s_pts, 1)

            keep_q(0)
            for n in range(B + TURN):
                if n < B:
                    act.wait_ge(s_mx, 2 * n + 2)
                    if n >= 2 * B4:
                        m = n - 2 * B4
                        act.wait_ge(s_pt, turned(m))
                        act.wait_ge(s_pb, m + 1)
                    for u in range(2):
                        act.activation(pr[:, n // B4 % 2, u, n % B4, :], S[:, n % 2, u, :], ACT.Exp,
                                       bias=nb[:, n % 4, u:u + 1], scale=-1.0,
                                       accum_out=rs[:, n % 8, u:u + 1]).then_inc(s_exp, 1)
                if n % B4 == 1 and n // B4 + 1 < NT:
                    keep_q(n // B4 + 1)
                m = n - TURN
                if m >= 0:
                    if m % B4 == 0:
                        keep_probs(turned(m) - 2)
                    keep_probs(turned(m) - 1)

        @block.vector
        def _(dve):
            ix = [0]

            def step(ins):
                ix[0] += 1
                ins.then_inc(s_ix, 1)
                dve.wait_ge(s_ix, ix[0])

            tt, ts, stt, cp = dve.tensor_tensor, dve.tensor_scalar, dve.scalar_tensor_tensor, dve.tensor_copy

            dve.wait_ge(s_lens, 16)
            dve.wait_ge(s_set, 3)
            step(cp(lens[:, :], lens_i[:, :]))
            step(ts(first[:, :], lens[:, :], float(WINDOW - 1), 0.0, ALU.subtract, ALU.max))
            step(cp(first_i[:, :], first[:, :]))
            ts(slot_i[:, 0, :], first_i[:, :], 4, None, ALU.arith_shift_right)
            ts(slot_i[:, 1, :], first_i[:, :], 15, None, ALU.bitwise_and)
            ts(slot_i[:, 2, :], lens_i[:, :], 4, None, ALU.arith_shift_right)
            step(ts(slot_i[:, 3, :], lens_i[:, :], 15, None, ALU.bitwise_and))
            step(cp(slot[:, :, :], slot_i[:, :, :]))
            dve.wait_ge(s_cst0, 16)
            step(tt(sel[:, 0:3, 0:SEQ_U], slot[:, 0, :].rearrange("p (u b) -> p u b", b=SEQ_U),
                    C("unit_seq").unsqueeze(1).broadcast_to([P, 3, SEQ_U]), ALU.mult))
            dve.tensor_reduce(pick[:, 0:3], sel[:, 0:3, 0:SEQ_U], AX.X, ALU.add)
            step(tt(sel[:, 3, 0:B], slot[:, 2, 0:B], C("wr_seq"), ALU.mult))
            step(dve.tensor_reduce(pick[:, 3:4], sel[:, 3, 0:B], AX.X, ALU.add))
            ts(tidx[:, 0:3], pick[:, 0:3], C("unit_blk"), float(SLOTS - 1), ALU.add, ALU.min)
            step(ts(tidx[:, 3:4], pick[:, 3:4], C("wr_blk"), float(SLOTS - 1), ALU.add, ALU.min))
            tt(tidx_i[:, 0:3], tidx[:, 0:3], C("unit_row"), ALU.add)
            step(tt(tidx_i[:, 3:4], tidx[:, 3:4], C("wr_row"), ALU.add))
            dve.sem_inc(s_tidx, 1)

            step(tt(hi[:, :], lens[:, 0:B], first[:, 0:B], ALU.subtract))
            ts(hi[:, :], hi[:, :], -1.0, (WINDOW - 1) / 2, ALU.mult, ALU.add).then_inc(s_ix, 1)
            ix[0] += 1
            dve.wait_ge(s_ix, ix[0])
            ts(hi[:, :], hi[:, :], C("in_tile"), None, ALU.subtract).then_inc(s_hi, 1)

            step(tt(sel8[:, :, :], lens[:, 0:B].rearrange("p (n b) -> p n b", b=B4),
                    C("quad").unsqueeze(1).broadcast_to([P, NT, B4]), ALU.mult))
            step(dve.tensor_reduce(pos[:, :], sel8[:, :, :], AX.X, ALU.add))
            step(ts(pos[:, :], pos[:, :], C("in_tile"), None, ALU.add))
            for k in range(2):
                tt(ang[:, :, k, :], pos[:, :].unsqueeze(2).broadcast_to([P, NT, HD // 2]),
                   C("inv").unsqueeze(1).broadcast_to([P, NT, HD // 2]), ALU.mult).then_inc(s_ix, 1)
            ix[0] += 2
            dve.wait_ge(s_ix, ix[0])
            step(ts(turns[:, :, :, :], ang[:, :, :, :], float(1 / (2 * np.pi)), None, ALU.mult))
            step(ts(turns[:, :, 1, :], turns[:, :, 1, :], 0.25, None, ALU.add))
            step(ts(turns[:, :, :, :], turns[:, :, :, :], ROUND, None, ALU.add))
            step(ts(turns[:, :, :, :], turns[:, :, :, :], ROUND, None, ALU.subtract))
            fl = lambda a: a[:, :, :, :].rearrange("p n k e -> p (n k e)")
            for c in (TWO_PI_HI, TWO_PI_MID, TWO_PI_LO):
                step(stt(fl(ang), fl(turns), -float(c), fl(ang), ALU.mult, ALU.add))
            step(ts(ang[:, :, 1, :], ang[:, :, 1, :], float(np.pi / 2), None, ALU.add))
            step(ts(ang[:, :, :, :], ang[:, :, :, :], PI_SAFE, -PI_SAFE, ALU.min, ALU.max))
            dve.sem_inc(s_an, 1)

            def masks(g):
                dve.wait_ge(s_dist, B4 * (g + 1))
                ts(mask[:, B4 * g:B4 * g + B4, :], dist(g), (WINDOW / 2) ** 2, -BIG, ALU.is_ge, ALU.mult).then_inc(s_mask, 1)

            for g in range(NT // 2):
                masks(g)
            dve.wait_ge(s_wt, 2)
            cp(AT[:, :, :], bank[1][:, 0:D].rearrange("p (c o) -> p c o", c=KC)).then_inc(s_wtD, 1)
            cp(BT[:, :], bank[1][:, D:2 * D]).then_inc(s_wtD, 1)
            dve.wait_ge(s_wt, 4)
            for kc in range(KC):
                cp(WqT[:, kc, :, :].rearrange("p s (g d) -> p s g d", g=G),
                   bank[3][:, kc * D:(kc + 1) * D].rearrange("p (g s d) -> p s g d", g=G, s=GS)).then_inc(s_wtD, 1)

            dve.wait_ge(s_adp, 16)
            dve.wait_ge(s_scal, 16)
            step(cp(amask[:, :], adp_i[:, :]))
            ts(amask[:, :], amask[:, :], C("adapter"), scal[:, 0:1], ALU.is_equal, ALU.mult).then_inc(s_am, 1)

            for h in range(2):
                n4 = slice(4 * h, 4 * h + 4)
                dve.wait_ge(s_mixw, 16)
                for t in range(4 * h, 4 * h + 4):
                    tt(mix[:, t, :].rearrange("p (q d) -> p q d", q=B4),
                       mixw[:, t, :].unsqueeze(1).broadcast_to([P, B4, T]),
                       C("quad").unsqueeze(2).broadcast_to([P, B4, T]), ALU.mult).then_inc(s_ix, 1)
                ix[0] += 4
                dve.wait_ge(s_ix, ix[0])
                tt(mix[:, n4, :], mix[:, n4, :], ident.unsqueeze(1).broadcast_to([P, 4, P]), ALU.add).then_inc(s_mix, 1)

            dve.wait_ge(s_tab, 64)
            for u in range(4):
                n = UNITS[u][1] * WB if u < 3 else NWI
                cp(tab[0:n, u:u + 1], tab_i[0:n, u:u + 1]).then_inc(s_ix, 1)
            ix[0] += 4
            dve.wait_ge(s_ix, ix[0])
            for u in range(4):
                n = UNITS[u][1] * WB if u < 3 else NWI
                ts(diag[0:n, u, 0:n], C("ident", n, 0, n), tab[0:n, u:u + 1], None, ALU.mult).then_inc(s_diag, 1)
            step(tt(sel[0:NWI, 0, 0:B], slot[0:NWI, 3, 0:B], C("wr_seq", NWI), ALU.mult))
            step(dve.tensor_reduce(pick[0:NWI, 4:5], sel[0:NWI, 0, 0:B], AX.X, ALU.add))
            step(ts(wr[0:NWI, 0, :], C("wr_off", NWI), pick[0:NWI, 4:5], None, ALU.subtract))
            step(ts(wr[0:NWI, 1, :], wr[0:NWI, 0, :], 0.0, None, ALU.is_ge))
            step(stt(wr[0:NWI, 2, :], wr[0:NWI, 0, :], float(T - 1), wr[0:NWI, 1, :], ALU.is_le, ALU.mult))
            step(ts(wr[0:NWI, 0, :], wr[0:NWI, 0, :], C("wr_new", NWI), None, ALU.add))
            dve.wait_ge(s_brd, 1)
            stt(later[0:NWI, :], bank[7][0:NWI, B * WB:B * WB + NWI], tab[0:NWI, 3:4], C("later", NWI),
                ALU.is_equal, ALU.mult).then_inc(s_inr, 1)
            ts(hit[0:NWI, :], bank[7][0:NWI, 0:B * WB], tab[0:NWI, 3:4], None, ALU.is_equal).then_inc(s_inr, 1)
            dve.wait_ge(s_cnt, 1)
            step(stt(wr[0:NWI, 1, :], bank[7][0:NWI, 448:448 + BLOCK], 0.0, wr[0:NWI, 2, :], ALU.is_equal, ALU.mult))
            tt(wr[0:NWI, 3, :], wr[0:NWI, 1, :], wr[0:NWI, 0, :], ALU.mult).then_inc(s_val, 1)
            step(tt(sel[0:B, 1, 0:B], slot[0:B, 1, 0:B], C("ident", B, 0, B), ALU.mult))
            step(dve.tensor_reduce(pick[0:B, 5:6], sel[0:B, 1, 0:B], AX.X, ALU.add))
            step(cp(bits_i[0:B, 0:1], pick[0:B, 5:6]))
            for k in (1, 2, 3):
                ts(bits_i[0:B, k:k + 1], bits_i[0:B, 0:1], 1 << k, None, ALU.bitwise_and).then_inc(s_ix, 1)
            ix[0] += 3
            dve.wait_ge(s_ix, ix[0])
            step(ts(bits_i[0:B, 0:1], bits_i[0:B, 0:1], 1, None, ALU.bitwise_and))
            step(cp(bits[0:B, :], bits_i[0:B, :]))
            for k in (1, 2, 3):
                ts(bits[0:B, k:k + 1], bits[0:B, k:k + 1], 1.0 / (1 << k), None, ALU.mult).then_inc(s_ix, 1)
            ix[0] += 3
            dve.wait_ge(s_ix, ix[0])
            for h in range(2):
                dve.wait_ge(s_l0, 2 * h + 2)
                cp(x1T[:, 1, 512 * h:512 * h + 512], bank[(6, 1)[h]][:, :]).then_inc(s_x1D, 1)
            dve.wait_ge(s_am, 1)
            for h in range(2):
                dve.wait_ge(s_xa, h + 1)
                tt(xaT[:, 512 * h:512 * h + 512].rearrange("p (b t) -> p b t", t=T),
                   bank[2 + h][:, :].rearrange("p (b t) -> p b t", t=T),
                   amask[:, 16 * h:16 * h + 16].unsqueeze(2).broadcast_to([P, 16, T]), ALU.mult).then_inc(s_xas, 1)

            dve.wait_ge(s_nrow, 1)
            step(stt(rows[:, 0, :], bank[7][0:B, 0:WROWS], 0.0, C("win_row", B), ALU.is_equal, ALU.mult))
            step(tt(rows[:, 1, :], rows[:, 0, :], bank[7][0:B, 0:WROWS], ALU.add))
            a, w = 1, WROWS
            for k in (3, 2, 1, 0):
                w -= 1 << k
                step(tt(rows[:, 2, 0:w], rows[:, a, (1 << k):(1 << k) + w], rows[:, a, 0:w], ALU.subtract))
                step(stt(rows[:, 1 - a, 0:w], rows[:, 2, 0:w], bits[0:B, k:k + 1], rows[:, a, 0:w], ALU.mult, ALU.add))
                a = 1 - a
            assert a == 1
            dve.sem_inc(s_rowf, 1)

            dve.wait_ge(s_norms, 32)
            step(ts(ns[:, :, 0, :], ns[:, :, 0, :], 1.0, None, ALU.add))
            step(cp(ns[:, :, 1, :], ns[:, :, 0, :]))
            step(ts(ns[:, :, 1, HD // 2:HD], ns[:, :, 1, HD // 2:HD], -1.0, None, ALU.mult))
            dve.wait_ge(s_tr, 1)
            for j in range(2):
                for k in range(2):
                    for hf in range(2):
                        e = slice(HD // 2 * hf, HD // 2 * hf + HD // 2)
                        tt(rot[:, j, k, :, e], trig[:, :, 1 - k, :],
                           ns[:, j, k, e].unsqueeze(1).broadcast_to([P, NT, HD // 2]), ALU.mult).then_inc(s_rt, 1)
            dve.wait_ge(s_rt, 8)

            for g in range(NT // 2, NT):
                masks(g)
            for k in range(4):
                oc, h = k % 2, k // 2
                dve.wait_ge(s_l1, k + 1)
                if k == 0:
                    dve.wait_ge(s_x1A, 2)
                    dve.wait_ge(s_x1D, 2)
                tt(x2T[:, oc, 512 * h:512 * h + 512], bank[(4, 5, 6, 0)[k]][:, :],
                   x1T[:, oc, 512 * h:512 * h + 512], ALU.add).then_inc(s_x2, 1)
            dve.wait_ge(s_rowT, 1)
            ts(rowA[:, :], bank[7][:, 200:200 + B], 1.0, None, ALU.subtract).then_inc(s_rowi, 1)
            for q in range(B4):
                ts(rowB[T * q:T * q + T, :], bank[7][0:KB, 240:240 + B].rearrange("p (n b) -> p n b", b=B4)[:, :, q],
                   1.0, None, ALU.subtract).then_inc(s_rowi, 1)

            nstep = [0]

            def nlink(ins):
                nstep[0] += 1
                ins.then_inc(s_nstep, 1)
                dve.wait_ge(s_nstep, nstep[0])

            def norm_rotate(j, h, nh, heads, sq, cosp, sinp, ss, rr, kept, scaled, sin_done, done):
                def sums():
                    dve.wait_ge(s_kvk if j else s_qk, kept)
                    dve.tensor_reduce(ss[:, 4 * h:4 * h + 4, :], sq, AX.X, ALU.add).then_inc(s_ss, 1)

                def scale_cos():
                    dve.wait_ge(s_rt2, h + 1 if j else h + 3)
                    nlink(dve.reciprocal(rr[:, 4 * h:4 * h + 4, :], rr[:, 4 * h:4 * h + 4, :]))
                    tt(heads, heads, rr[:, 4 * h:4 * h + 4, :].unsqueeze(3).broadcast_to([P, 4, nh, HD]), ALU.mult).then_inc(scaled, 1)
                    dve.wait_ge(scaled, h + 1)
                    nlink(tt(cosp, heads, table_of(j, 0, h, nh), ALU.mult))

                def add_halves():
                    e0, e1 = slice(0, HD // 2), slice(HD // 2, HD)
                    dve.wait_ge(sin_done, h + 1)
                    tt(heads[:, :, :, e0], cosp[:, :, :, e0], sinp[:, :, :, e1], ALU.add).then_inc(s_nstep, 1)
                    tt(heads[:, :, :, e1], cosp[:, :, :, e1], sinp[:, :, :, e0], ALU.add).then_inc(s_nstep, 1)
                    nstep[0] += 2
                    dve.wait_ge(s_nstep, nstep[0])
                    dve.sem_inc(done, 1)

                return sums, scale_cos, add_halves

            for j in (1, 0):
                if j:
                    parts = [norm_rotate(1, h, G, k_heads(h), k_sq(h), k_sq(h), k_sin(h), ssk, rstdk, 4 * h + 4, s_kn, s_ksin, s_kready)
                             for h in range(2)]
                else:
                    parts = [norm_rotate(0, h, H, q_heads(h), q_sq(h), q_cos(h), q_sin(h), ssq, rstd, 4 * h + 4, s_qn, s_qsin, s_qready)
                             for h in range(2)]
                parts[0][0]()
                parts[0][1]()
                parts[1][0]()
                parts[0][2]()
                parts[1][1]()
                parts[1][2]()

            def keep_k(g):
                dve.wait_ge(s_kt, 2 * g + 1)
                if g >= 2:
                    dve.wait_ge(s_sc, B4 * (g - 1))
                cp(KT[:, g % 2, :, 0:P], bank[1][:, :].rearrange("p (b r) -> p b r", b=B4)).then_inc(s_kta, 1)

            keep_k(0)
            dve.wait_ge(s_mask, NT)

            def normalise(n):
                dve.wait_ge(s_exp, 2 * n + 2)
                dve.reciprocal(ri[:, n % 8, :], rs[:, n % 8, :]).then_inc(s_ri, 1)
                dve.wait_ge(s_ri, n + 1)
                for u in range(2):
                    e_ = pr[:, n // B4 % 2, u, n % B4, 0:P]
                    ts(e_, e_, ri[:, n % 8, u:u + 1], None, ALU.mult).then_inc(s_pn, 1)

            for n in range(B + TAIL):
                if n < B:
                    dve.wait_ge(s_sc, n + 1)
                    if n >= 2:
                        dve.wait_ge(s_exp, 2 * n - 2)
                    for u in range(2):
                        dve.tensor_tensor_reduce(S[:, n % 2, u, :], bank[3 + n % 2][:, u * KEYS:(u + 1) * KEYS], mask[:, n, :],
                                                 -SCALE, 3e38, ALU.add, ALU.min, nb[:, n % 4, u:u + 1]).then_inc(s_mx, 1)
                k = n - PV
                if 0 <= k < B and k % B4 == B4 - 1:
                    g = k // B4
                    dve.wait_ge(s_pv, k + 1)
                    if g >= 2:
                        dve.wait_ge(s_wo, g - 1)
                    cp(oT[:, g % 2, :, :, :].rearrange("p b s t -> p b (s t)"),
                       bank[0][:, 0:D].rearrange("p (b c) -> p b c", b=B4)).then_inc(s_ot, 1)
                if 2 <= n < B + 2:
                    normalise(n - 2)
                if n % B4 == 1 and n // B4 + 1 < NT:
                    keep_k(n // B4 + 1)
                k = n - PV - 2
                if 0 <= k < B and k % B4 == B4 - 1:
                    g = k // B4
                    dve.wait_ge(s_wo, g + 1)
                    if g >= 2:
                        dve.wait_ge(s_l3, g - 1)
                    tt(x3T[:, g % 2, :, :], bank[7][:, 0:D].rearrange("p (c r) -> p c r", c=KC),
                       x2T[:, :, g * P:(g + 1) * P], ALU.add).then_inc(s_x3, 1)
                k = n - PV - 4
                if 0 <= k < B and k % B4 == B4 - 1:
                    g = k // B4
                    dve.wait_ge(s_l3, g + 1)
                    dve.wait_ge(s_be[g % 2], 16 * B4 * (g // 2 + 1))
                    if g >= 2:
                        dve.wait_ge(s_out[g % 2], 16 * (g // 2))
                    tt(res[:, g % 2, :], bank[7][:, D:2 * D], be[:, g % 2, :], ALU.add).then_inc(s_res, 1)

        @block.tensor
        def _(pe):
            mm, tr = pe.matmul, pe.transpose
            pe.wait_ge(s_cst, 16)

            def turn_square(j, src, m, waits):
                for s, v in waits:
                    pe.wait_ge(s, v)
                for kc in range(KC):
                    for oc in range(KC):
                        c0 = kc * D + oc * P
                        i_ = tr(bank[j][:, c0:c0 + P], src[:, oc, m, kc * P:(kc + 1) * P], ident)
                i_.then_inc(s_wt, 1)

            turn_square(0, nat, 0, [(s_w1, 16)])
            pe.wait_ge(s_ab, 48)
            for kc in range(KC):
                tr(bank[1][:, kc * P:(kc + 1) * P], natA[:, kc * P:(kc + 1) * P], ident)
            for oc in range(KC):
                i_ = tr(bank[1][:, D + oc * P:D + (oc + 1) * P], natB[:, oc, :], ident)
            i_.then_inc(s_wt, 1)
            turn_square(2, nat, 2, [(s_kvw, 32)])
            turn_square(3, nat, 1, [(s_qw, 16)])
            pe.wait_ge(s_wo_l, 16 * KC * GS)
            for s in range(GS):
                for oc in range(KC):
                    c0 = s * D + oc * P
                    i_ = tr(bank[4][:, c0:c0 + P],
                            nat[:, oc, 3, s * KV:(s + 1) * KV], ident)
            i_.then_inc(s_wt, 1)

            for h in range(2):
                pe.wait_ge(s_mix, h + 1)
                pe.wait_ge(s_x, 16 * (h + 1)) if h == 0 else pe.wait_ge(s_x, 32)
                if h == 0:
                    pe.wait_ge(s_x, 32)
                for c in range(KC):
                    if h == 1:
                        pe.wait_ge(*((s_wtA, 1), (s_wtD, 2))[c])
                    for t in range(4):
                        i_ = mm(bank[(5, 6, 0, 1)[2 * h + c]][:, t * P:(t + 1) * P], xin[:, 4 * h + t, c * P:(c + 1) * P],
                                mix[:, 4 * h + t, :], start=True, stop=True)
                    i_.then_inc(s_l0, 1)

            pe.wait_ge(s_diag, 4)
            pe.wait_ge(s_set, 3)
            for u in range(4):
                n = UNITS[u][1] * WB if u < 3 else NWI
                c0 = UNITS[u][0] * WB if u < 3 else B * WB
                i_ = mm(bank[7][0:NWI, c0:c0 + n], ones[0:n, 0:NWI], diag[0:n, u, 0:n], start=True, stop=True)
            i_.then_inc(s_brd, 1)
            pe.wait_ge(s_inr, 2)
            mm(bank[7][0:NWI, 448:448 + BLOCK], later[0:NWI, :], wr[0:NWI, 2, :], start=True, stop=True).then_inc(s_cnt, 1)

            pe.wait_ge(s_wtD, 4)
            pe.wait_ge(s_wtA, 3)
            for h in range(2):
                pe.wait_ge(s_x1A, h + 1)
                pe.wait_ge(s_x1D, h + 1)
                for kc in range(KC):
                    i_ = mm(bank[2 + h][:, :], AT[:, kc, :], x1T[:, kc, 512 * h:512 * h + 512], start=(kc == 0), stop=(kc == KC - 1))
                i_.then_inc(s_xa, 1)
            pe.wait_ge(s_val, 1)
            hits = hit[0:NWI, :].rearrange("p (b j) -> p b j", j=WB)
            for j in range(WB):
                i_ = mm(bank[7][0:B, j * BLOCK:(j + 1) * BLOCK], hits[:, :, j], wr[0:NWI, 3, :], start=True, stop=True)
            i_.then_inc(s_nrow, 1)
            for k in range(4):
                oc, h = k % 2, k // 2
                o = bank[(4, 5, 6, 0)[k]]
                for kc in range(KC):
                    mm(o[:, :], W1T[:, kc, oc * P:(oc + 1) * P], x1T[:, kc, 512 * h:512 * h + 512], start=(kc == 0), stop=False)
                pe.wait_ge(s_xas, h + 1)
                mm(o[:, :], BT[:, oc * P:(oc + 1) * P], xaT[:, 512 * h:512 * h + 512], start=False, stop=True).then_inc(s_l1, 1)
            pe.wait_ge(s_rowf, 1)
            tr(bank[7][:, 200:200 + B], rows[:, 1, 0:P], ident[0:B, 0:B])
            tr(bank[7][0:KB, 240:240 + B], rows[:, 1, P:KEYS], ident[0:B, 0:B]).then_inc(s_rowT, 1)

            for t in range(NT):
                if t % 4 == 0:
                    pe.wait_ge(s_x2, 2 * (t // 4 + 1))
                if t == 0:
                    pe.wait_ge(s_xas, 2)
                for kc in range(KC):
                    i_ = mm(bank[1 + t // 2][:, (t % 2) * D:(t % 2) * D + D], x2T[:, kc, t * P:(t + 1) * P], WkvT[:, kc, :],
                            start=(kc == 0), stop=(kc == KC - 1))
                if t % 2:
                    i_.then_inc(s_kvp, 1)
            for t in range(NT):
                if t == 6:
                    pe.wait_ge(s_rowi, 5)
                for kc in range(KC):
                    i_ = mm(bank[(5, 6, 0, 7)[t // 2]][:, (t % 2) * D:(t % 2) * D + D], x2T[:, kc, t * P:(t + 1) * P],
                            WqT[:, kc, :, :].rearrange("p s c -> p (s c)"), start=(kc == 0), stop=(kc == KC - 1))
                if t % 2:
                    i_.then_inc(s_qp, 1)

            def turn_k(g):
                if g >= 1:
                    pe.wait_ge(s_kta, g)
                else:
                    pe.wait_ge(s_kvk, NT)
                for j in range(B4):
                    b = B4 * g + j
                    pe.wait_ge(s_kvA[b % NA], 16 * (b // NA + 1))
                    i_ = tr(bank[1][:, j * P:(j + 1) * P], kvA[:, b % NA, 0:KV], ident)
                i_.then_inc(s_kt, 1)
                if g >= 1:
                    pe.wait_ge(s_qt, G * g)
                pe.wait_ge(s_kvB[g], 16)
                tr(bank[2][:, 0:P], kvB(g, slice(0, KV)), ident)
                pe.wait_ge(s_qready, g // 4 + 1)
                for s in range(GS):
                    i_ = tr(bank[2][:, P + s * P:P + (s + 1) * P], qn[:, g, s * KV:(s + 1) * KV], ident)
                i_.then_inc(s_kt, 1)

            def scores(n):
                g, j = divmod(n, B4)
                if j == 0:
                    pe.wait_ge(s_kta, g + 1)
                    pe.wait_ge(s_ktb, g + 1)
                    pe.wait_ge(s_qt, G * (g + 1))
                if n >= 2:
                    pe.wait_ge(s_mx, 2 * (n - 1))
                for u in range(2):
                    i_ = mm(bank[3 + n % 2][:, u * KEYS:(u + 1) * KEYS],
                            QBD[:, g % 2, j, 2 * u:2 * u + 2, :].rearrange("p g c -> p (g c)"), KT[:, g % 2, j, :],
                            start=True, stop=True)
                i_.then_inc(s_sc, 1)

            def turn_probs(seq):
                g, j = divmod(seq, B4 + 1)
                if j == 0:
                    pe.wait_ge(s_pb, B4 * (g + 1))
                else:
                    pe.wait_ge(s_pn, 2 * (B4 * g + j))
                if seq >= 2:
                    pe.wait_ge(s_pts, seq - 1)
                else:
                    pe.wait_ge(s_qk, 4)
                for u in range(2):
                    src = prB[:, g % 2, u, :, :].rearrange("p b r -> p (b r)") if j == 0 else pr[:, g % 2, u, j - 1, 0:P]
                    i_ = tr(bank[5 + seq % 2][:, u * P:(u + 1) * P], src, ident)
                i_.then_inc(s_pt, 1)

            def pv(n):
                g, j = divmod(n, B4)
                pe.wait_ge(s_pts, g * (B4 + 1) + j + 2)
                if j == 0:
                    if g:
                        pe.wait_ge(s_ot, g)
                    else:
                        pe.wait_ge(s_qk, 6)
                pe.wait_ge(s_vbd, g + 1)
                for k in range(G):
                    o = bank[0][HD * k:HD * k + HD, j * GS * T:(j + 1) * GS * T]
                    c = slice(GS * T * (k % 2), GS * T * (k % 2) + GS * T)
                    v = slice(KV + HD * k, KV + HD * k + HD)
                    mm(o, kvA[:, n % NA, v], PTA[:, n % 3, k // 2, c], start=True, stop=False)
                    i_ = mm(o, VBD[:, g % 2, j, HD * k:HD * k + HD], PTB[:, g % 2, k // 2, c], start=False, stop=True)
                i_.then_inc(s_pv, 1)

            def project(g):
                pe.wait_ge(s_ot, g + 1)
                if g:
                    pe.wait_ge(s_res, g)
                else:
                    pe.wait_ge(s_qk, 8)
                for oc in range(KC):
                    for s in range(GS):
                        i_ = mm(bank[7][:, oc * P:(oc + 1) * P], WoT[:, s, oc * P:(oc + 1) * P], oT[:, g % 2, :, s, :],
                                start=(s == 0), stop=(s == GS - 1))
                i_.then_inc(s_wo, 1)

            def layer3(g):
                pe.wait_ge(s_x3, g + 1)
                o = bank[7][:, D:2 * D]
                for kc in range(KC):
                    mm(o[:, kc * P:(kc + 1) * P], x3T[:, g % 2, kc, :], ident, start=(kc == 0), stop=False, skip_group_check=True)
                for j in range(B4):
                    b = B4 * g + j
                    pe.wait_ge(s_we[b % NE], 16 * (b // NE + 1))
                    for kc in range(KC):
                        i_ = mm(o[T * j:T * j + T, :], x3T[:, g % 2, kc, T * j:T * j + T], We[:, b % NE, kc, :],
                                start=False, stop=(kc == KC - 1), skip_group_check=True)
                i_.then_inc(s_l3, 1)

            turn_k(0)
            scores(0)
            for n in range(B + TAIL):
                if n + 1 < B:
                    scores(n + 1)
                if n % B4 == 1 and n // B4 + 1 < NT:
                    turn_k(n // B4 + 1)
                m = n - TURN
                if 0 <= m < B:
                    if m % B4 == 0:
                        turn_probs(turned(m) - 2)
                    turn_probs(turned(m) - 1)
                if 0 <= n - PV < B:
                    pv(n - PV)
                k = n - PV - 1
                if 0 <= k < B and k % B4 == B4 - 1:
                    project(k // B4)
                k = n - PV - 3
                if 0 <= k < B and k % B4 == B4 - 1:
                    layer3(k // B4)


_INS = ["x", "itok_B_1_198", "itok_B_0_6", "itok_Bx257_0_4111", "itok_B_37_3939", "itok_B_0_15", "L0_cond_weights",
        "L1_cond_W", "L1_cond_A", "L1_cond_Bm", "L1_cond_scalings", "L2_cond_Wq", "L2_cond_Wk", "L2_cond_Wv",
        "L2_cond_Wo", "L2_cond_q_norm_scale", "L2_cond_k_norm_scale", "L2_cond_k_blocks", "L2_cond_v_blocks",
        "L3_cond_W", "L3_cond_b"]


def kernel(**inputs):
    from concourse import bacc
    from concourse.bass_utils import run_bass_kernel_spmd

    nc = bacc.Bacc("TRN2", target_bir_lowering=False, num_devices=1)
    arrays, args = {}, []
    for name in _INS:
        a = np.ascontiguousarray(inputs[name])
        arrays[f"in_{name}"] = a
        args.append(nc.dram_tensor(f"in_{name}", a.shape, mybir.dt.from_np(a.dtype), kind="ExternalInput").ap())
    c = Columns().data
    arrays["in_consts"] = c
    args.append(nc.dram_tensor("in_consts", c.shape, F32, kind="ExternalInput").ap())
    args.append(nc.dram_tensor("out", (B, T, D), F32, kind="ExternalOutput").ap())
    program(nc, *args)
    r = run_bass_kernel_spmd(nc, [arrays], core_ids=[0])
    return r.results[0]["out"]
```

```python
from contextlib import ExitStack

import numpy as np

import concourse.bass as bass
from concourse import mybir
from concourse.alu_op_type import AluOpType as ALU

ACT = mybir.ActivationFunctionType
AX = mybir.AxisListType
F32 = mybir.dt.float32
BF16 = mybir.dt.bfloat16
I32 = mybir.dt.int32

P = 128
B, T, D = 32, 32, 256
KC = D // P
B4 = P // T
NT = B // B4
H, G, HD = 8, 4, 32
GS = H // G
KV = G * HD
BLOCK, WINDOW, NBLK = 16, 128, 257
SLOTS = 257
NPOOL = 16 * NBLK
SCALE = float(D) ** -0.5
EPS = 1e-6
THETA = 10000.0
ADAPTERS, RANK = 8, 16
EXPERTS = 16
NCOND = 200
KEYS = 160
KB = KEYS - P
WB = 11
WROWS = WB * BLOCK
SEQ_U = 11
UNITS = [(0, 11), (11, 11), (22, 10)]
NW = 3
NWI = B * NW
NEW0 = 0
WIN0 = NEW0 + B * T
NROWS = WIN0 + B * WROWS
BIG = 1e30
TURN, PV = 6, 7
KEEP_O, PROJECT, KEEP_X3, LAYER3, RESULT = (PV + i for i in (1, 1, 2, 2, 3))
TAIL = RESULT + 1
AHEAD = 10
TWO_PI_HI = 6.28125
TWO_PI_MID = 0.0019350051879882812
TWO_PI_LO = 2 * np.pi - TWO_PI_HI - TWO_PI_MID
ROUND = 12582912.0
PI_SAFE = 3.1415925


EARLY = ("unit_seq", "unit_blk", "unit_row", "wr_seq", "wr_blk", "wr_row", "in_tile", "quad", "inv")
LATE = ("ident",)


class Columns:

    def __init__(self):
        p = np.arange(P)
        r = lambda a: np.broadcast_to(np.asarray(a, np.float32), (P, len(a)))
        c = lambda a: np.asarray(a, np.float32).reshape(P, -1)
        half = HD // 2
        inv = (np.float32(1.0) / np.power(np.float32(THETA), np.arange(half, dtype=np.float32) / np.float32(half)))
        parts = {
            "ident": np.eye(P),
            "iota": r(np.arange(KEYS)),
            "inv": r(inv.astype(np.float32)),
            "quad": c([[q // T == j for j in range(B4)] for q in p]),
            "in_tile": c(p % T),
            "unit_seq": c([[q // WB == j for j in range(SEQ_U)] for q in p]),
            "unit_blk": c(p % WB),
            "unit_row": c([[min(u * SEQ_U + q // WB, B - 1) * SLOTS for u in range(3)] for q in p]),
            "wr_seq": c([[q // NW == j for j in range(B)] for q in p]),
            "wr_blk": c(p % NW),
            "wr_row": c(np.minimum(p // NW, B - 1) * SLOTS),
            "wr_off": c([[BLOCK * (q % NW) + o for o in range(BLOCK)] for q in p]),
            "wr_new": c(p // NW * T + NEW0 + 1),
            "later": c([[i < q for i in range(NWI)] for q in p]),
            "win_row": c([[WIN0 + q * WROWS + x + 1 for x in range(WROWS)] for q in p]),
            "adapter": c(p // RANK),
        }
        self.at, self.data, n = {}, [], 0
        parts = {**{k: parts[k] for k in EARLY}, **{k: v for k, v in parts.items() if k not in EARLY}}
        for k, v in parts.items():
            v = np.asarray(v, np.float32)
            if k == LATE[0]:
                self.early = n
            self.at[k] = (n, n + v.shape[1])
            self.data.append(v)
            n += v.shape[1]
        self.width = n
        self.data = np.ascontiguousarray(np.concatenate(self.data, 1), np.float32)


def program(nc, x, cond, adapter_idx, table, kv_lens, expert_ids, W0, W1, A1, B1, s1, Wq, Wk, Wv, Wo, q_norm, k_norm,
            k_blocks, v_blocks, W3, b3, consts, out):
    cols = Columns()
    ctx = ExitStack()

    def sb(name, shape, dt=F32):
        return ctx.enter_context(nc.sbuf_tensor(name, shape, dt))

    def sem(name):
        return ctx.enter_context(nc.semaphore(name))

    with ctx:
        mix_rows = nc.dram_tensor("mix_rows", [B * T, T], F32).ap()
        kv_rows = nc.dram_tensor("kv_rows", [NROWS, 2 * KV], F32).ap()

        cst = sb("cst", [P, cols.width])

        def C(name, parts=P, a=0, b=None):
            lo, hi = cols.at[name]
            return cst[0:parts, lo + a:(hi if b is None else lo + b)]

        ident = C("ident")
        ones = sb("ones", [P, P])
        nat = sb("nat", [P, 2, 4, D])
        natA = sb("natA", [P, D])
        natB = sb("natB", [P, KC, P])
        W1T = sb("W1T", [P, KC, D])
        WkvT = sb("WkvT", [P, KC, 2 * KV])
        WqT = sb("WqT", [P, KC, GS, KV])
        WoT = sb("WoT", [P, GS, D])
        AT = sb("AT", [P, KC, P])
        BT = sb("BT", [P, D])
        xin = sb("xin", [P, NT, D])
        mixw = sb("mixw", [P, NT, T])
        kvn = sb("kvn", [P, NT, 2 * KV])
        mixg = kvn[0:B, 0:4, :].rearrange("p n c -> p (n c)")
        mix = sb("mix", [P, NT, P])
        x1T = sb("x1T", [P, KC, B * T])
        qn = x1T[:, :, :].rearrange("p c r -> p (c r)").rearrange("p (n c) -> p n c", n=NT)
        x2T = sb("x2T", [P, KC, B * T])
        xaT = sb("xaT", [P, B * T])

        ksq = sb("ksq", [P, NT, KV])
        ksn = sb("ksn", [P, NT, KV])
        wo_s = ksn[:, 0:4, :].rearrange("p (c s) d -> p c (s d)", c=KC)
        ssq = sb("ssq", [P, NT, H])
        rstd = sb("rstd", [P, NT, H])
        ssk = sb("ssk", [P, NT, G])
        rstdk = sb("rstdk", [P, NT, G])
        eps = sb("eps", [P, 1])
        warm = sb("warm", [P, 2])
        blk = sb("blk", [P, 3, BLOCK * KV])
        qsq, qcs, qsn = (blk[:, i, :].rearrange("p (n c) -> p n c", n=NT) for i in range(3))
        blkp = sb("blkp", [P, 2, BLOCK * KV])
        lens_i = sb("lens_i", [P, B + 1], I32)
        cond_i = sb("cond_i", [B, 1], I32)
        adp_i = sb("adp_i", [P, B], I32)
        ids_i = sb("ids_i", [1, B], I32)
        lens = sb("lens", [P, B + 1])
        first = sb("first", [P, B + 1])
        first_i = sb("first_i", [P, B + 1], I32)
        slot_i = sb("slot_i", [P, 4, B + 1], I32)
        slot = sb("slot", [P, 4, B + 1])
        sel = sb("sel", [P, 4, B + 1])
        pick = sb("pick", [P, 8])
        tidx = sb("tidx", [P, 4])
        tidx_i = sb("tidx_i", [P, 4], I32)
        tab_i = sb("tab_i", [P, 4], I32)
        tab = sb("tab", [P, 4])
        diag = sb("diag", [P, 4, P])
        hit = sb("hit", [P, B * WB])
        later = sb("later", [P, NWI])
        wr = sb("wr", [P, 4, BLOCK])
        bits_i = sb("bits_i", [P, 4], I32)
        bits = sb("bits", [P, 4])
        rows = sb("rows", [B, 3, WROWS])
        rowA = sb("rowA", [P, B], I32)
        rowB = sb("rowB", [P, NT], I32)
        scal = sb("scal", [P, 1])
        amask = sb("amask", [P, B])
        pos = sb("pos", [P, NT])
        ang = sb("ang", [P, NT, 2, HD // 2])
        turns = sb("turns", [P, NT, 2, HD // 2])
        trig = sb("trig", [P, NT, 2, HD // 2])
        ns = sb("ns", [P, 2, 2, HD])
        rot = sb("rot", [P, 2, 2, NT, HD])
        hi = sb("hi", [P, B])
        sel8 = sb("sel8", [P, NT, B4])
        mask = sb("mask", [P, B, KEYS], BF16)
        kvA_own = sb("kvA", [P, B // 2, 2 * KV])
        over_blkp = blkp[:, :, :].rearrange("p i c -> p (i c)").rearrange("p (b c) -> p b c", c=2 * KV)
        kvA = lambda b, c: kvA_own[:, b, c] if b < B // 2 else over_blkp[:, b - B // 2, c]
        kvB_own = sb("kvB", [P, NT // 2, 2 * KV])
        VBD = xin[:, 0:4, :].rearrange("p n c -> p (n c)").rearrange("p (g b c) -> p g b c", g=2, b=B4)
        kvB = lambda g, c: kvB_own[:, g, c] if g < NT // 2 else xin[:, g, c]
        KT = sb("KT", [P, 2, B4, KEYS])
        QBD = sb("QBD", [P, 2, B4, G, GS * T])
        S = sb("S", [P, 2, 2, KEYS])
        pr = sb("pr", [P, 2, 2, B4, KEYS])
        prB = sb("prB", [P, 2, 2, B4, KB])
        nb = sb("nb", [P, 4, 2])
        rs = sb("rs", [P, 8, 2])
        ri = sb("ri", [P, 8, 2])
        PTA = sb("PTA", [P, 3, 2, P])
        PTB = sb("PTB", [P, 2, 2, P])
        oT = sb("oT", [P, 2, B4, GS, T])
        x3T = sb("x3T", [P, 2, KC, P])
        NE = 8
        We_own = sb("We", [P, NE // 2, KC, D])
        over_kvn = kvn[:, :, :].rearrange("p n c -> p (n c)").rearrange("p (e c o) -> p e c o", e=NE // 2, c=KC)
        We = lambda b: (We_own if b % NE < NE // 2 else over_kvn)[:, b % (NE // 2), :, :]
        be = sb("be", [P, 2, D])
        res = nat[:, :, 0, :]
        over_kvA = kvA_own[:, :, :].rearrange("p b c -> p (b c)").rearrange("p (i c) -> p i c", i=2)
        blk_src = [blk[:, 0, :], blk[:, 1, :], blk[:, 2, :], over_kvA[:, 0, :], over_kvA[:, 1, :],
                   kvn[:, :, :].rearrange("p n c -> p (n c)")]
        blk_dst = [blkp[:, 0, :], blkp[:, 1, :], QBD[:, :, :, :, :].rearrange("p i b g c -> p (i b g c)"),
                   We_own[:, :, :, :].rearrange("p e c o -> p (e c o)"), blk[:, 2, :], over_kvA[:, 0, :]]
        bank = [ctx.enter_context(nc.psum_tensor(f"bank{i}", [P, 512], F32)) for i in range(8)]

        s_cst0 = sem("cst_early_loaded")
        s_cst, s_lens, s_cond, s_adp, s_ids, s_x = (sem(f"{n}_loaded") for n in ("cst", "lens", "cond", "adp", "ids", "x"))
        s_scal, s_norms, s_wo_l, s_wop = (sem(n) for n in ("scal_loaded", "norms_loaded", "wo_loaded", "wo_permuted"))
        s_w1, s_ab, s_kvw, s_qw = sem("w1_loaded"), sem("ab_loaded"), sem("kvw_loaded"), sem("qw_loaded")
        s_set = sem("constants_set")
        s_ix = sem("index_step")
        s_tidx, s_tab = sem("table_index_ready"), sem("table_read")
        s_mixg, s_mixs, s_mixw = sem("mix_gathered"), sem("mix_in_scratch"), sem("mix_loaded")
        s_kn, s_ksin, s_qn, s_qsin, s_pb = (sem(n) for n in ("k_scaled", "k_sines_ready", "q_scaled", "q_sines_ready", "tail_probs_ready"))
        s_bl = [sem(f"blocks_loaded{i}") for i in range(6)]
        s_perm = [sem(f"blocks_permuted{i}") for i in range(6)]
        s_winw = [sem(f"window_written{i}") for i in range(6)]
        s_neww = sem("new_rows_written")
        s_diag, s_brd, s_inr, s_cnt, s_val, s_nrow, s_rowf, s_rowT, s_rowi = (
            sem(n) for n in ("diagonals_ready", "blocks_broadcast", "writers_ready", "overwrites_counted", "valid_ready",
                             "new_row_found", "key_rows_ready", "key_rows_turned", "key_rows_int"))
        s_wt, s_wtA, s_wtD = sem("weights_turned"), sem("weights_kept_act"), sem("weights_kept_dve")
        s_mix = sem("mix_ready")
        s_l0, s_x1A, s_x1D = sem("mix_done"), sem("x1_kept_act"), sem("x1_kept_dve")
        s_xa, s_xas, s_l1, s_x2 = sem("down_done"), sem("down_kept"), sem("layer1_done"), sem("x2_kept")
        s_am = sem("adapter_mask_ready")
        s_kvp, s_kvk, s_qp, s_qk = sem("kv_projected"), sem("kv_kept"), sem("q_projected"), sem("q_kept")
        s_an, s_tr, s_rt = sem("angles_ready"), sem("trig_ready"), sem("rotation_ready")
        s_ss, s_rt2, s_nstep, s_kready, s_qready = (
            sem(n) for n in ("sums_ready", "roots_ready", "norm_step", "k_ready", "q_ready"))
        s_hi, s_dist, s_mask = sem("middles_ready"), sem("distances_ready"), sem("masks_ready")
        dist = lambda g: pr[:, g % 2, g // 2 % 2, :, :]
        s_kvA = [sem(f"kvA_loaded{i}") for i in range(B)]
        s_kvB = [sem(f"kvB_loaded{i}") for i in range(NT)]
        s_kt, s_kta, s_ktb, s_qt = sem("k_turned"), sem("kA_kept"), sem("kB_kept"), sem("q_kept_diagonal")
        s_qz, s_vbd = sem("q_diagonal_zeroed"), sem("v_diagonal_ready")
        s_sc, s_mx, s_exp, s_ri, s_pn = (sem(n) for n in (
            "scores_ready", "max_ready", "exp_ready", "inverse_ready", "probs_ready"))
        s_pt, s_pts, s_pv, s_ot = sem("probs_turned"), sem("probs_kept"), sem("pv_done"), sem("o_kept")
        s_wo, s_x3, s_l3, s_res = sem("wo_done"), sem("x3_kept"), sem("layer3_done"), sem("result_ready")
        s_we = [sem(f"expert_loaded{i}") for i in range(NE)]
        s_be = [sem(f"expert_bias_loaded{i}") for i in range(2)]
        s_out = [sem(f"output_written{i}") for i in range(2)]

        k_heads = lambda h: kvn[:, 4 * h:4 * h + 4, 0:KV].rearrange("p n (h e) -> p n h e", e=HD)
        q_heads = lambda h: qn[:, 4 * h:4 * h + 4, :].rearrange("p n (h e) -> p n h e", e=HD)
        of_half = lambda t, h: t[:, 4 * h:4 * h + 4, :].rearrange("p n (h e) -> p n h e", e=HD)
        k_sq, k_sin = (lambda h: of_half(ksq, h)), (lambda h: of_half(ksn, h))
        q_sq, q_cos, q_sin = (lambda h: of_half(qsq, h)), (lambda h: of_half(qcs, h)), (lambda h: of_half(qsn, h))
        table_of = lambda j, k, h, nh: rot[:, j, k, 4 * h:4 * h + 4, :].unsqueeze(2).broadcast_to([P, 4, nh, HD])
        turned = lambda m: m // B4 * (B4 + 1) + m % B4 + 2

        block = ctx.enter_context(nc.Block())

        pool_k = k_blocks.rearrange("n g o d -> n (g o d)")
        pool_v = v_blocks.rearrange("n g o d -> n (g o d)")
        LOADS = [(u, kv) for u in range(3) for kv in range(2)]

        def permutation(i):
            n = UNITS[LOADS[i][0]][1] * WB
            return (blk_src[i][0:n, :].rearrange("p (g o d) -> p g o d", g=G, o=BLOCK),
                    blk_dst[i][0:n, :].rearrange("p (o g d) -> p g o d", o=BLOCK, g=G))

        out_rows = out.rearrange("b t d -> (b t) d").rearrange("(n p) d -> n p d", p=P)

        @block.sync
        def _(sp):
            sp.dma_start(cond_i[:, :], cond.unsqueeze(1)).then_inc(s_cond, 16)
            sp.dma_start(lens_i[:, 0:B], kv_lens.partition_broadcast(P)).then_inc(s_lens, 16)
            sp.dma_start(cst[:, 0:cols.early], consts[:, 0:cols.early]).then_inc(s_cst0, 16)
            sp.dma_start(nat[:, :, 0, :], W1.rearrange("(c p) d -> p c d", p=P)).then_inc(s_w1, 16)
            for j in range(2):
                sp.dma_start(xin[:, 4 * j:4 * j + 4, :],
                             x.rearrange("b c t -> (b c) t").rearrange("(n p) t -> p n t", p=P)[:, 4 * j:4 * j + 4, :]) \
                    .then_inc(s_x, 16)
            sp.wait_ge(s_mixg, 16)
            sp.dma_start(mix_rows.rearrange("(b c) d -> b (c d)", c=T), mixg).then_inc(s_mixs, 16)
            sp.wait_ge(s_mixs, 16)
            sp.dma_start(mixw[:, :, :], mix_rows.rearrange("(n p) d -> p n d", p=P)).then_inc(s_mixw, 16)
            sp.dma_start(nat[:, 0, 2, :], Wk).then_inc(s_kvw, 16)
            sp.dma_start(nat[:, 1, 2, :], Wv).then_inc(s_kvw, 16)
            sp.dma_start(nat[:, :, 1, :], Wq.rearrange("(c p) d -> p c d", p=P)).then_inc(s_qw, 16)

            for i in (2, 0, 3, 4, 1, 5):
                u, kv = LOADS[i]
                b0, nb_ = UNITS[u]
                n = nb_ * WB
                sp.wait_ge(s_perm[i], 1)
                r0 = WIN0 + b0 * WROWS
                dst = kv_rows[r0:r0 + n * BLOCK, kv * KV:(kv + 1) * KV].rearrange("(p o) c -> p o c", o=BLOCK)
                sp.dma_start(dst, blk_dst[i][0:n, :].rearrange("p (o c) -> p o c", o=BLOCK)).then_inc(s_winw[i], 16)
            for h in range(2):
                sp.wait_ge(s_kready, h + 1)
                r0 = NEW0 + 4 * h * P
                sp.dma_start(kv_rows[r0:r0 + 4 * P, :].rearrange("(j p) c -> p j c", p=P),
                             kvn[:, 4 * h:4 * h + 4, :]).then_inc(s_neww, 16)
            sp.wait_ge(s_ids, 16)
            sp.wait_ge(s_winw[3], 16)

            def expert(b):
                g = b // B4
                if b >= NE:
                    sp.wait_ge(s_l3, (b - NE) // B4 + 1)
                if g >= 2 and b % B4 == 0:
                    sp.wait_ge(s_res, g - 1)
                if b == NE // 2:
                    sp.wait_ge(s_neww, 32)
                e = sp.value_load(ids_i[0:1, b:b + 1], min_val=0, max_val=EXPERTS - 1)
                sp.dma_start(We(b), W3[bass.ds(e, 1), :, :].rearrange("e (c p) o -> p (e c) o", p=P)) \
                    .then_inc(s_we[b % NE], 16)
                sp.dma_start(be[T * (b % B4):T * (b % B4) + T, g % 2, :],
                             b3[bass.ds(e, 1), :].rearrange("e o -> (e o)").partition_broadcast(T)).then_inc(s_be[g % 2], 16)

            for b in range(NE):
                expert(b)
            nxt = NE
            for g in range(NT):
                while nxt < B and (nxt - NE) // B4 <= g and not (nxt % B4 == 0 and nxt // B4 - 1 > g):
                    expert(nxt)
                    nxt += 1
                sp.wait_ge(s_res, g + 1)
                sp.dma_start(out_rows[g], res[:, g % 2, :]).then_inc(s_out[g % 2], 16)
            assert nxt == B
            for j in range(2):
                sp.wait_ge(s_out[j], 16 * NT // 2)

        @block.gpsimd
        def _(pool):
            pool.memset(ones[:, :], 1.0).then_inc(s_set, 1)
            pool.memset(lens_i[:, B:B + 1], 0).then_inc(s_set, 1)
            pool.memset(eps[:, :], EPS).then_inc(s_set, 1)
            pool.wait_ge(s_cond, 16)
            pool.indirect_dma_start(out=mixg, out_offset=None, in_=W0.rearrange("s c d -> s (c d)"),
                                    in_offset=bass.IndirectOffsetOnAxis(ap=cond_i[:, :], axis=0)).then_inc(s_mixg, 16)
            pool.wait_ge(s_tidx, 1)
            table_1 = table.rearrange("b s -> (b s)").unsqueeze(1)
            for u in range(4):
                n = UNITS[u][1] * WB if u < 3 else NWI
                pool.indirect_dma_start(out=tab_i[0:n, u:u + 1], out_offset=None, in_=table_1,
                                        in_offset=bass.IndirectOffsetOnAxis(ap=tidx_i[0:n, u:u + 1], axis=0)).then_inc(s_tab, 16)
            pool.wait_ge(s_wo_l, 16)
            for oc in range(KC):
                pool.tensor_copy(wo_s[:, oc, :].rearrange("p (s g d) -> p g s d", s=GS, g=G),
                                 nat[:, oc, 3, :].rearrange("p (g s d) -> p g s d", g=G, s=GS)).then_inc(s_wop, 1)
            pool.wait_ge(s_tab, 64)

            def load_blocks(i):
                u, kv = LOADS[i]
                n = UNITS[u][1] * WB
                pool.indirect_dma_start(out=blk_src[i][0:n, :], out_offset=None, in_=(pool_k, pool_v)[kv],
                                        in_offset=bass.IndirectOffsetOnAxis(ap=tab_i[0:n, u:u + 1], axis=0)).then_inc(s_bl[i], 16)

            for i in range(5):
                load_blocks(i)
            pool.wait_ge(s_mixs, 16)
            load_blocks(5)
            for i in (0, 1):
                src, dst = permutation(i)
                pool.wait_ge(s_bl[i], 16)
                pool.tensor_copy(dst, src).then_inc(s_perm[i], 1)
            pool.wait_ge(s_winw[2], 16)
            pool.memset(QBD[:, :, :, :, :], 0.0).then_inc(s_qz, 1)
            for h in range(2):
                pool.wait_ge(s_kn, h + 1)
                pool.tensor_tensor(k_sin(h), k_heads(h), table_of(1, 1, h, G), ALU.mult).then_inc(s_ksin, 1)


            def gather_b(g):
                pool.indirect_dma_start(out=kvB(g, slice(0, 2 * KV)), out_offset=None, in_=kv_rows,
                                        in_offset=bass.IndirectOffsetOnAxis(ap=rowB[:, g:g + 1], axis=0)) \
                    .then_inc(s_kvB[g], 16)

            def gather_a(b):
                if b % B4 == 0:
                    gather_b(b // B4)
                pool.indirect_dma_start(out=kvA(b, slice(0, 2 * KV)), out_offset=None, in_=kv_rows,
                                        in_offset=bass.IndirectOffsetOnAxis(ap=rowA[:, b:b + 1], axis=0)).then_inc(s_kvA[b], 16)

            pool.wait_ge(s_l0, 4)
            pool.wait_ge(s_rowi, 5)
            for i in range(6):
                pool.wait_ge(s_winw[i], 16)
            pool.wait_ge(s_neww, 32)
            for b in range(AHEAD):
                gather_a(b)
            pool.wait_ge(s_cst0, 16)
            for n in range(B + 2):
                if n % B4 == 3 and n // B4 < NT:
                    g = n // B4
                    pool.wait_ge(s_kvB[g], 16)
                    if g >= 2:
                        pool.wait_ge(s_pv, B4 * (g - 1))
                    pool.tensor_tensor(VBD[:, g % 2, :, :],
                                       kvB(g, slice(KV, 2 * KV)).unsqueeze(1).broadcast_to([P, B4, KV]),
                                       C("quad").unsqueeze(2).broadcast_to([P, B4, KV]), ALU.mult).then_inc(s_vbd, 1)
                if n >= 2:
                    k = n - 2
                    pool.wait_ge(s_ri, k + 1)
                    pool.tensor_tensor(prB[:, k // B4 % 2, :, k % B4, :], pr[:, k // B4 % 2, :, k % B4, P:KEYS],
                                       ri[:, k % 8, :].unsqueeze(2).broadcast_to([P, 2, KB]), ALU.mult).then_inc(s_pb, 1)
                if n + AHEAD < B:
                    gather_a(n + AHEAD)

        @block.scalar
        def _(act):
            act.dma_start(cst[:, cols.early:], consts[:, cols.early:]).then_inc(s_cst, 16)
            act.dma_start(natA[:, :], A1.rearrange("n r d -> (n r) d")).then_inc(s_ab, 16)
            for oc in range(KC):
                act.dma_start(natB[:, oc, :].rearrange("p (n r) -> p n r", r=RANK),
                              B1[:, oc * P:(oc + 1) * P, :].rearrange("n o r -> o n r")).then_inc(s_ab, 16)
            act.dma_start(adp_i[:, :], adapter_idx.partition_broadcast(P)).then_inc(s_adp, 16)
            act.dma_start(scal[:, :], s1.unsqueeze(1).broadcast_to([ADAPTERS, RANK])).then_inc(s_scal, 16)
            for j, w in enumerate((q_norm, k_norm)):
                act.dma_start(ns[:, j, 0, :], w.partition_broadcast(P)).then_inc(s_norms, 16)
            act.dma_start(ids_i[:, :], expert_ids.unsqueeze(0)).then_inc(s_ids, 16)
            act.dma_start(nat[:, :, 3, :], Wo.rearrange("(c p) d -> p c d", p=P)).then_inc(s_wo_l, 16)

            def keep_weights(nth, src, dst):
                act.wait_ge(s_wt, nth)
                act.copy(dst[:, :, :], bank[src][:, :].rearrange("p (c o) -> p c o", c=2)).then_inc(s_wtA, 1)

            keep_weights(1, 0, W1T)
            for h in range(2):
                act.wait_ge(s_l0, 2 * h + 1)
                act.copy(x1T[:, 0, 512 * h:512 * h + 512], bank[(5, 0)[h]][:, :]).then_inc(s_x1A, 1)
            keep_weights(3, 4, WoT)
            for i in (2, 3):
                src, dst = permutation(i)
                act.wait_ge(s_bl[i], 16)
                act.copy(dst, src).then_inc(s_perm[i], 1)
            keep_weights(4, 2, WkvT)


            def distances(g):
                if g == 0:
                    act.wait_ge(s_hi, 1)
                if g >= 4:
                    act.wait_ge(s_mask, g - 3)
                for j in range(B4):
                    act.activation(dist(g)[:, j, :], C("iota"), ACT.Square, bias=hi[:, B4 * g + j:B4 * g + j + 1]) \
                        .then_inc(s_dist, 1)

            act.wait_ge(s_an, 1)
            act.activation(trig[:, :, :, :], ang[:, :, :, :], ACT.Sin).then_inc(s_tr, 1)
            act.wait_ge(s_set, 3)
            act.activation(warm[:, 0:1], eps[:, 0:1], ACT.Sqrt)
            act.wait_ge(s_cst0, 16)
            act.wait_ge(s_cst, 16)
            distances(0)
            distances(1)
            act.wait_ge(s_perm[5], 1)
            for t in range(NT // 2):
                act.wait_ge(s_kvp, t + 1)
                b_ = bank[1 + t][:, :].rearrange("p (j c) -> p j c", j=2)
                act.copy(kvn[:, 2 * t:2 * t + 2, :], b_).then_inc(s_kvk, 1)
                act.activation(ksq[:, 2 * t:2 * t + 2, :], b_[:, :, 0:KV], ACT.Square).then_inc(s_kvk, 1)
                if t % 2:
                    h = t // 2
                    act.wait_ge(s_ss, h + 1)
                    act.activation(rstdk[:, 4 * h:4 * h + 4, :], ssk[:, 4 * h:4 * h + 4, :], ACT.Sqrt,
                                   bias=eps[:, 0:1], scale=1.0 / HD).then_inc(s_rt2, 1)
                    distances(2 + h)
            act.wait_ge(s_perm[0], 1)
            act.wait_ge(s_perm[1], 1)
            act.wait_ge(s_winw[4], 16)
            for t in range(NT // 2):
                act.wait_ge(s_qp, t + 1)
                b_ = bank[(5, 6, 0, 7)[t]][:, :].rearrange("p (j c) -> p j c", j=2)
                act.copy(qn[:, 2 * t:2 * t + 2, :], b_).then_inc(s_qk, 1)
                act.activation(qsq[:, 2 * t:2 * t + 2, :], b_, ACT.Square).then_inc(s_qk, 1)
                if t % 2:
                    h = t // 2
                    if h:
                        distances(6)
                        distances(7)
                    act.wait_ge(s_ss, h + 3)
                    act.activation(rstd[:, 4 * h:4 * h + 4, :], ssq[:, 4 * h:4 * h + 4, :], ACT.Sqrt,
                                   bias=eps[:, 0:1], scale=1.0 / HD).then_inc(s_rt2, 1)
                    if h == 0:
                        distances(4)
                        distances(5)
            act.activation(warm[:, 1:2], eps[:, 0:1], ACT.Exp)

            def keep_q(g):
                act.wait_ge(s_kt, 2 * g + 2)
                if g >= 2:
                    act.wait_ge(s_sc, B4 * (g - 1))
                act.copy(KT[:, g % 2, :, P:KEYS], bank[2][:, 0:P].rearrange("p (b r) -> p b r", b=B4)).then_inc(s_ktb, 1)
                if g == 0:
                    act.wait_ge(s_qz, 1)
                for k in range(G):
                    q = slice(HD * k, HD * k + HD)
                    act.copy(QBD[q, g % 2, :, k, :].rearrange("p b (s t) -> p s b t", s=GS),
                             bank[2][q, P:P + 2 * P].rearrange("p (s b t) -> p s b t", s=GS, b=B4)).then_inc(s_qt, 1)

            def keep_probs(seq):
                g, j = divmod(seq, B4 + 1)
                act.wait_ge(s_pt, seq + 1)
                if j == 0:
                    if g >= 2:
                        act.wait_ge(s_pv, B4 * (g - 1))
                    dst = PTB[:, g % 2, :, :]
                else:
                    m = B4 * g + j - 1
                    if m >= 3:
                        act.wait_ge(s_pv, m - 2)
                    dst = PTA[:, m % 3, :, :]
                act.copy(dst, bank[5 + seq % 2][:, 0:2 * P].rearrange("p (u r) -> p u r", u=2)).then_inc(s_pts, 1)

            keep_q(0)
            for n in range(B + TURN):
                if n < B:
                    act.wait_ge(s_mx, 2 * n + 2)
                    if n >= 2 * B4:
                        m = n - 2 * B4
                        act.wait_ge(s_pt, turned(m))
                        act.wait_ge(s_pb, m + 1)
                    for u in range(2):
                        act.activation(pr[:, n // B4 % 2, u, n % B4, :], S[:, n % 2, u, :], ACT.Exp,
                                       bias=nb[:, n % 4, u:u + 1], scale=-1.0,
                                       accum_out=rs[:, n % 8, u:u + 1]).then_inc(s_exp, 1)
                if n % B4 == 1 and n // B4 + 1 < NT:
                    keep_q(n // B4 + 1)
                m = n - TURN
                if m >= 0:
                    if m % B4 == 0:
                        keep_probs(turned(m) - 2)
                    keep_probs(turned(m) - 1)

        @block.vector
        def _(dve):
            ix = [0]

            def step(ins):
                ix[0] += 1
                ins.then_inc(s_ix, 1)
                dve.wait_ge(s_ix, ix[0])

            tt, ts, stt, cp = dve.tensor_tensor, dve.tensor_scalar, dve.scalar_tensor_tensor, dve.tensor_copy

            dve.wait_ge(s_lens, 16)
            dve.wait_ge(s_set, 3)
            step(cp(lens[:, :], lens_i[:, :]))
            step(ts(first[:, :], lens[:, :], float(WINDOW - 1), 0.0, ALU.subtract, ALU.max))
            step(cp(first_i[:, :], first[:, :]))
            ts(slot_i[:, 0, :], first_i[:, :], 4, None, ALU.arith_shift_right)
            ts(slot_i[:, 1, :], first_i[:, :], 15, None, ALU.bitwise_and)
            ts(slot_i[:, 2, :], lens_i[:, :], 4, None, ALU.arith_shift_right)
            step(ts(slot_i[:, 3, :], lens_i[:, :], 15, None, ALU.bitwise_and))
            step(cp(slot[:, :, :], slot_i[:, :, :]))
            dve.wait_ge(s_cst0, 16)
            step(tt(sel[:, 0:3, 0:SEQ_U], slot[:, 0, :].rearrange("p (u b) -> p u b", b=SEQ_U),
                    C("unit_seq").unsqueeze(1).broadcast_to([P, 3, SEQ_U]), ALU.mult))
            dve.tensor_reduce(pick[:, 0:3], sel[:, 0:3, 0:SEQ_U], AX.X, ALU.add)
            step(tt(sel[:, 3, 0:B], slot[:, 2, 0:B], C("wr_seq"), ALU.mult))
            step(dve.tensor_reduce(pick[:, 3:4], sel[:, 3, 0:B], AX.X, ALU.add))
            ts(tidx[:, 0:3], pick[:, 0:3], C("unit_blk"), float(SLOTS - 1), ALU.add, ALU.min)
            step(ts(tidx[:, 3:4], pick[:, 3:4], C("wr_blk"), float(SLOTS - 1), ALU.add, ALU.min))
            tt(tidx_i[:, 0:3], tidx[:, 0:3], C("unit_row"), ALU.add)
            step(tt(tidx_i[:, 3:4], tidx[:, 3:4], C("wr_row"), ALU.add))
            dve.sem_inc(s_tidx, 1)

            step(tt(hi[:, :], lens[:, 0:B], first[:, 0:B], ALU.subtract))
            ts(hi[:, :], hi[:, :], -1.0, (WINDOW - 1) / 2, ALU.mult, ALU.add).then_inc(s_ix, 1)
            ix[0] += 1
            dve.wait_ge(s_ix, ix[0])
            ts(hi[:, :], hi[:, :], C("in_tile"), None, ALU.subtract).then_inc(s_hi, 1)

            step(tt(sel8[:, :, :], lens[:, 0:B].rearrange("p (n b) -> p n b", b=B4),
                    C("quad").unsqueeze(1).broadcast_to([P, NT, B4]), ALU.mult))
            step(dve.tensor_reduce(pos[:, :], sel8[:, :, :], AX.X, ALU.add))
            step(ts(pos[:, :], pos[:, :], C("in_tile"), None, ALU.add))
            for k in range(2):
                tt(ang[:, :, k, :], pos[:, :].unsqueeze(2).broadcast_to([P, NT, HD // 2]),
                   C("inv").unsqueeze(1).broadcast_to([P, NT, HD // 2]), ALU.mult).then_inc(s_ix, 1)
            ix[0] += 2
            dve.wait_ge(s_ix, ix[0])
            step(ts(turns[:, :, :, :], ang[:, :, :, :], float(1 / (2 * np.pi)), None, ALU.mult))
            step(ts(turns[:, :, 1, :], turns[:, :, 1, :], 0.25, None, ALU.add))
            step(ts(turns[:, :, :, :], turns[:, :, :, :], ROUND, None, ALU.add))
            step(ts(turns[:, :, :, :], turns[:, :, :, :], ROUND, None, ALU.subtract))
            fl = lambda a: a[:, :, :, :].rearrange("p n k e -> p (n k e)")
            for c in (TWO_PI_HI, TWO_PI_MID, TWO_PI_LO):
                step(stt(fl(ang), fl(turns), -float(c), fl(ang), ALU.mult, ALU.add))
            step(ts(ang[:, :, 1, :], ang[:, :, 1, :], float(np.pi / 2), None, ALU.add))
            step(ts(ang[:, :, :, :], ang[:, :, :, :], PI_SAFE, -PI_SAFE, ALU.min, ALU.max))
            dve.sem_inc(s_an, 1)

            def masks(g):
                dve.wait_ge(s_dist, B4 * (g + 1))
                ts(mask[:, B4 * g:B4 * g + B4, :], dist(g), (WINDOW / 2) ** 2, -BIG, ALU.is_ge, ALU.mult).then_inc(s_mask, 1)

            dve.wait_ge(s_wt, 2)
            cp(AT[:, :, :], bank[1][:, 0:D].rearrange("p (c o) -> p c o", c=KC)).then_inc(s_wtD, 1)
            cp(BT[:, :], bank[1][:, D:2 * D]).then_inc(s_wtD, 1)
            for h in range(2):
                n4 = slice(4 * h, 4 * h + 4)
                dve.wait_ge(s_mixw, 16)
                dve.wait_ge(s_cst, 16)
                for t in range(4 * h, 4 * h + 4):
                    tt(mix[:, t, :].rearrange("p (q d) -> p q d", q=B4),
                       mixw[:, t, :].unsqueeze(1).broadcast_to([P, B4, T]),
                       C("quad").unsqueeze(2).broadcast_to([P, B4, T]), ALU.mult).then_inc(s_ix, 1)
                ix[0] += 4
                dve.wait_ge(s_ix, ix[0])
                tt(mix[:, n4, :], mix[:, n4, :], ident.unsqueeze(1).broadcast_to([P, 4, P]), ALU.add).then_inc(s_mix, 1)

            dve.wait_ge(s_adp, 16)
            dve.wait_ge(s_scal, 16)
            step(cp(amask[:, :], adp_i[:, :]))
            ts(amask[:, :], amask[:, :], C("adapter"), scal[:, 0:1], ALU.is_equal, ALU.mult).then_inc(s_am, 1)

            def scale_down(h):
                dve.wait_ge(s_xa, h + 1)
                tt(xaT[:, 512 * h:512 * h + 512].rearrange("p (b t) -> p b t", t=T),
                   bank[2 + h][:, :].rearrange("p (b t) -> p b t", t=T),
                   amask[:, 16 * h:16 * h + 16].unsqueeze(2).broadcast_to([P, 16, T]), ALU.mult).then_inc(s_xas, 1)

            def residual(k):
                oc, h = k % 2, k // 2
                dve.wait_ge(s_l1, k + 1)
                if k == 0:
                    dve.wait_ge(s_x1A, 2)
                    dve.wait_ge(s_x1D, 2)
                tt(x2T[:, oc, 512 * h:512 * h + 512], bank[(4, 5, 6, 0)[k]][:, :],
                   x1T[:, oc, 512 * h:512 * h + 512], ALU.add).then_inc(s_x2, 1)

            def permute(i, source_of):
                src, dst = permutation(i)
                dve.wait_ge(s_bl[i], 16)
                dve.wait_ge(s_perm[source_of], 1)
                cp(dst, src).then_inc(s_perm[i], 1)

            dve.wait_ge(s_tab, 64)
            for u in range(4):
                n = UNITS[u][1] * WB if u < 3 else NWI
                cp(tab[0:n, u:u + 1], tab_i[0:n, u:u + 1]).then_inc(s_ix, 1)
            ix[0] += 4
            dve.wait_ge(s_ix, ix[0])
            for u in range(4):
                n = UNITS[u][1] * WB if u < 3 else NWI
                ts(diag[0:n, u, 0:n], C("ident", n, 0, n), tab[0:n, u:u + 1], None, ALU.mult).then_inc(s_diag, 1)
            for h in range(2):
                dve.wait_ge(s_l0, 2 * h + 2)
                cp(x1T[:, 1, 512 * h:512 * h + 512], bank[(6, 1)[h]][:, :]).then_inc(s_x1D, 1)
            step(tt(sel[0:NWI, 0, 0:B], slot[0:NWI, 3, 0:B], C("wr_seq", NWI), ALU.mult))
            step(dve.tensor_reduce(pick[0:NWI, 4:5], sel[0:NWI, 0, 0:B], AX.X, ALU.add))
            step(ts(wr[0:NWI, 0, :], C("wr_off", NWI), pick[0:NWI, 4:5], None, ALU.subtract))
            step(ts(wr[0:NWI, 1, :], wr[0:NWI, 0, :], 0.0, None, ALU.is_ge))
            step(stt(wr[0:NWI, 2, :], wr[0:NWI, 0, :], float(T - 1), wr[0:NWI, 1, :], ALU.is_le, ALU.mult))
            step(ts(wr[0:NWI, 0, :], wr[0:NWI, 0, :], C("wr_new", NWI), None, ALU.add))
            dve.wait_ge(s_brd, 1)
            stt(later[0:NWI, :], bank[7][0:NWI, B * WB:B * WB + NWI], tab[0:NWI, 3:4], C("later", NWI),
                ALU.is_equal, ALU.mult).then_inc(s_inr, 1)
            ts(hit[0:NWI, :], bank[7][0:NWI, 0:B * WB], tab[0:NWI, 3:4], None, ALU.is_equal).then_inc(s_inr, 1)
            dve.wait_ge(s_am, 1)
            scale_down(0)
            dve.wait_ge(s_cnt, 1)
            step(stt(wr[0:NWI, 1, :], bank[7][0:NWI, 448:448 + BLOCK], 0.0, wr[0:NWI, 2, :], ALU.is_equal, ALU.mult))
            tt(wr[0:NWI, 3, :], wr[0:NWI, 1, :], wr[0:NWI, 0, :], ALU.mult).then_inc(s_val, 1)
            scale_down(1)
            step(tt(sel[0:B, 1, 0:B], slot[0:B, 1, 0:B], C("ident", B, 0, B), ALU.mult))
            step(dve.tensor_reduce(pick[0:B, 5:6], sel[0:B, 1, 0:B], AX.X, ALU.add))
            step(cp(bits_i[0:B, 0:1], pick[0:B, 5:6]))
            for k in (1, 2, 3):
                ts(bits_i[0:B, k:k + 1], bits_i[0:B, 0:1], 1 << k, None, ALU.bitwise_and).then_inc(s_ix, 1)
            ix[0] += 3
            dve.wait_ge(s_ix, ix[0])
            step(ts(bits_i[0:B, 0:1], bits_i[0:B, 0:1], 1, None, ALU.bitwise_and))
            step(cp(bits[0:B, :], bits_i[0:B, :]))
            for k in (1, 2, 3):
                ts(bits[0:B, k:k + 1], bits[0:B, k:k + 1], 1.0 / (1 << k), None, ALU.mult).then_inc(s_ix, 1)
            ix[0] += 3
            dve.wait_ge(s_ix, ix[0])
            residual(0)
            permute(4, 2)
            residual(1)
            dve.wait_ge(s_wt, 5)
            for kc in range(KC):
                cp(WqT[:, kc, :, :].rearrange("p s (g d) -> p s g d", g=G),
                   bank[3][:, kc * D:(kc + 1) * D].rearrange("p (g s d) -> p s g d", g=G, s=GS)).then_inc(s_wtD, 1)

            dve.wait_ge(s_nrow, 1)
            step(stt(rows[:, 0, :], bank[7][0:B, 0:WROWS], 0.0, C("win_row", B), ALU.is_equal, ALU.mult))
            step(tt(rows[:, 1, :], rows[:, 0, :], bank[7][0:B, 0:WROWS], ALU.add))
            a, w = 1, WROWS
            for k in (3, 2, 1, 0):
                w -= 1 << k
                step(tt(rows[:, 2, 0:w], rows[:, a, (1 << k):(1 << k) + w], rows[:, a, 0:w], ALU.subtract))
                step(stt(rows[:, 1 - a, 0:w], rows[:, 2, 0:w], bits[0:B, k:k + 1], rows[:, a, 0:w], ALU.mult, ALU.add))
                a = 1 - a
            assert a == 1
            dve.sem_inc(s_rowf, 1)
            permute(5, 3)
            residual(2)
            dve.wait_ge(s_norms, 32)
            step(ts(ns[:, :, 0, :], ns[:, :, 0, :], 1.0, None, ALU.add))
            step(cp(ns[:, :, 1, :], ns[:, :, 0, :]))
            step(ts(ns[:, :, 1, HD // 2:HD], ns[:, :, 1, HD // 2:HD], -1.0, None, ALU.mult))
            dve.wait_ge(s_tr, 1)
            for j in range(2):
                for k in range(2):
                    for hf in range(2):
                        e = slice(HD // 2 * hf, HD // 2 * hf + HD // 2)
                        tt(rot[:, j, k, :, e], trig[:, :, 1 - k, :],
                           ns[:, j, k, e].unsqueeze(1).broadcast_to([P, NT, HD // 2]), ALU.mult).then_inc(s_rt, 1)
            dve.wait_ge(s_rt, 8)

            nstep = [0]

            def nlink(ins):
                nstep[0] += 1
                ins.then_inc(s_nstep, 1)
                dve.wait_ge(s_nstep, nstep[0])

            def norm_rotate(j, h, nh, heads, sq, cosp, sinp, ss, rr, kept, scaled, sin_done, done):
                def sums():
                    dve.wait_ge(s_kvk if j else s_qk, kept)
                    dve.tensor_reduce(ss[:, 4 * h:4 * h + 4, :], sq, AX.X, ALU.add).then_inc(s_ss, 1)

                def scale():
                    dve.wait_ge(s_rt2, h + 1 if j else h + 3)
                    nlink(dve.reciprocal(rr[:, 4 * h:4 * h + 4, :], rr[:, 4 * h:4 * h + 4, :]))
                    tt(heads, heads, rr[:, 4 * h:4 * h + 4, :].unsqueeze(3).broadcast_to([P, 4, nh, HD]), ALU.mult).then_inc(scaled, 1)

                def cosines():
                    dve.wait_ge(scaled, h + 1)
                    nlink(tt(cosp, heads, table_of(j, 0, h, nh), ALU.mult))

                def sines():
                    if j == 0:
                        tt(sinp, heads, table_of(0, 1, h, nh), ALU.mult).then_inc(sin_done, 1)

                def add_halves():
                    e0, e1 = slice(0, HD // 2), slice(HD // 2, HD)
                    dve.wait_ge(sin_done, h + 1)
                    tt(heads[:, :, :, e0], cosp[:, :, :, e0], sinp[:, :, :, e1], ALU.add).then_inc(s_nstep, 1)
                    tt(heads[:, :, :, e1], cosp[:, :, :, e1], sinp[:, :, :, e0], ALU.add).then_inc(s_nstep, 1)
                    nstep[0] += 2
                    dve.wait_ge(s_nstep, nstep[0])
                    dve.sem_inc(done, 1)

                return sums, scale, cosines, sines, add_halves

            k_part = [norm_rotate(1, h, G, k_heads(h), k_sq(h), k_sq(h), k_sin(h), ssk, rstdk, 4 * h + 4, s_kn, s_ksin, s_kready)
                      for h in range(2)]
            q_part = [norm_rotate(0, h, H, q_heads(h), q_sq(h), q_cos(h), q_sin(h), ssq, rstd, 4 * h + 4, s_qn, s_qsin, s_qready)
                      for h in range(2)]
            SUMS, BY_ROOT, COS, SIN, ADD = range(5)
            k_part[0][SUMS]()
            residual(3)
            k_part[0][BY_ROOT]()
            k_part[0][COS]()
            dve.wait_ge(s_rowT, 1)
            ts(rowA[:, :], bank[7][:, 200:200 + B], 1.0, None, ALU.subtract).then_inc(s_rowi, 1)
            for q in range(B4):
                ts(rowB[T * q:T * q + T, :], bank[7][0:KB, 240:240 + B].rearrange("p (n b) -> p n b", b=B4)[:, :, q],
                   1.0, None, ALU.subtract).then_inc(s_rowi, 1)
            k_part[0][ADD]()
            masks(0)
            masks(1)
            k_part[1][SUMS]()
            masks(2)
            k_part[1][BY_ROOT]()
            k_part[1][COS]()
            k_part[1][ADD]()
            q_part[0][SUMS]()
            masks(3)
            q_part[0][BY_ROOT]()
            q_part[0][COS]()
            q_part[0][SIN]()
            q_part[0][ADD]()
            q_part[1][SUMS]()
            for g in range(NT // 2, NT):
                masks(g)

            def keep_k(g):
                dve.wait_ge(s_kt, 2 * g + 1)
                if g >= 2:
                    dve.wait_ge(s_sc, B4 * (g - 1))
                cp(KT[:, g % 2, :, 0:P], bank[1][:, :].rearrange("p (b r) -> p b r", b=B4)).then_inc(s_kta, 1)

            q_part[1][BY_ROOT]()
            keep_k(0)
            q_part[1][COS]()
            q_part[1][SIN]()
            dve.wait_ge(s_mask, NT)

            def normalise(n):
                dve.wait_ge(s_exp, 2 * n + 2)
                dve.reciprocal(ri[:, n % 8, :], rs[:, n % 8, :]).then_inc(s_ri, 1)
                dve.wait_ge(s_ri, n + 1)
                for u in range(2):
                    e_ = pr[:, n // B4 % 2, u, n % B4, 0:P]
                    ts(e_, e_, ri[:, n % 8, u:u + 1], None, ALU.mult).then_inc(s_pn, 1)

            for n in range(B + TAIL):
                if n < B:
                    dve.wait_ge(s_sc, n + 1)
                    if n >= 2:
                        dve.wait_ge(s_exp, 2 * n - 2)
                    for u in range(2):
                        dve.tensor_tensor_reduce(S[:, n % 2, u, :], bank[3 + n % 2][:, u * KEYS:(u + 1) * KEYS], mask[:, n, :],
                                                 -SCALE, 3e38, ALU.add, ALU.min, nb[:, n % 4, u:u + 1]).then_inc(s_mx, 1)
                k = n - KEEP_O
                if 0 <= k < B and k % B4 == B4 - 1:
                    g = k // B4
                    dve.wait_ge(s_pv, k + 1)
                    if g >= 2:
                        dve.wait_ge(s_wo, g - 1)
                    cp(oT[:, g % 2, :, :, :].rearrange("p b s t -> p b (s t)"),
                       bank[0][:, 0:D].rearrange("p (b c) -> p b c", b=B4)).then_inc(s_ot, 1)
                if 2 <= n < B + 2:
                    normalise(n - 2)
                if n == 3:
                    q_part[1][ADD]()
                if n % B4 == 1 and n // B4 + 1 < NT:
                    keep_k(n // B4 + 1)
                k = n - KEEP_X3
                if 0 <= k < B and k % B4 == B4 - 1:
                    g = k // B4
                    dve.wait_ge(s_wo, g + 1)
                    if g >= 2:
                        dve.wait_ge(s_l3, g - 1)
                    tt(x3T[:, g % 2, :, :], bank[7][:, 0:D].rearrange("p (c r) -> p c r", c=KC),
                       x2T[:, :, g * P:(g + 1) * P], ALU.add).then_inc(s_x3, 1)
                k = n - RESULT
                if 0 <= k < B and k % B4 == B4 - 1:
                    g = k // B4
                    dve.wait_ge(s_l3, g + 1)
                    dve.wait_ge(s_be[g % 2], 16 * B4 * (g // 2 + 1))
                    if g >= 2:
                        dve.wait_ge(s_out[g % 2], 16 * (g // 2))
                    tt(res[:, g % 2, :], bank[7][:, D:2 * D], be[:, g % 2, :], ALU.add).then_inc(s_res, 1)

        @block.tensor
        def _(pe):
            mm, tr = pe.matmul, pe.transpose
            pe.wait_ge(s_cst, 16)

            def turn_square(j, src, m, waits):
                for s, v in waits:
                    pe.wait_ge(s, v)
                for kc in range(KC):
                    for oc in range(KC):
                        c0 = kc * D + oc * P
                        i_ = tr(bank[j][:, c0:c0 + P], src[:, oc, m, kc * P:(kc + 1) * P], ident)
                i_.then_inc(s_wt, 1)

            turn_square(0, nat, 0, [(s_w1, 16)])
            pe.wait_ge(s_ab, 48)
            for kc in range(KC):
                tr(bank[1][:, kc * P:(kc + 1) * P], natA[:, kc * P:(kc + 1) * P], ident)
            for oc in range(KC):
                i_ = tr(bank[1][:, D + oc * P:D + (oc + 1) * P], natB[:, oc, :], ident)
            i_.then_inc(s_wt, 1)
            for h in range(2):
                pe.wait_ge(s_mix, h + 1)
                pe.wait_ge(s_x, 16 * (h + 1)) if h == 0 else pe.wait_ge(s_x, 32)
                if h == 0:
                    pe.wait_ge(s_x, 32)
                for c in range(KC):
                    if h == 1:
                        pe.wait_ge(*((s_wtA, 1), (s_wtD, 2))[c])
                    for t in range(4):
                        i_ = mm(bank[(5, 6, 0, 1)[2 * h + c]][:, t * P:(t + 1) * P], xin[:, 4 * h + t, c * P:(c + 1) * P],
                                mix[:, 4 * h + t, :], start=True, stop=True)
                    i_.then_inc(s_l0, 1)

            pe.wait_ge(s_wop, KC)
            for s in range(GS):
                for oc in range(KC):
                    c0 = s * D + oc * P
                    i_ = tr(bank[4][:, c0:c0 + P],
                            wo_s[:, oc, s * KV:(s + 1) * KV], ident)
            i_.then_inc(s_wt, 1)

            pe.wait_ge(s_wtD, 2)

            def down(h):
                pe.wait_ge(s_x1A, h + 1)
                pe.wait_ge(s_x1D, h + 1)
                for kc in range(KC):
                    i_ = mm(bank[2 + h][:, :], AT[:, kc, :], x1T[:, kc, 512 * h:512 * h + 512], start=(kc == 0), stop=(kc == KC - 1))
                i_.then_inc(s_xa, 1)

            down(0)
            pe.wait_ge(s_diag, 4)
            pe.wait_ge(s_set, 3)
            for u in range(4):
                n = UNITS[u][1] * WB if u < 3 else NWI
                c0 = UNITS[u][0] * WB if u < 3 else B * WB
                i_ = mm(bank[7][0:NWI, c0:c0 + n], ones[0:n, 0:NWI], diag[0:n, u, 0:n], start=True, stop=True)
            i_.then_inc(s_brd, 1)
            down(1)
            pe.wait_ge(s_inr, 2)
            mm(bank[7][0:NWI, 448:448 + BLOCK], later[0:NWI, :], wr[0:NWI, 2, :], start=True, stop=True).then_inc(s_cnt, 1)

            def layer1(k):
                oc, h = k % 2, k // 2
                o = bank[(4, 5, 6, 0)[k]]
                for kc in range(KC):
                    mm(o[:, :], W1T[:, kc, oc * P:(oc + 1) * P], x1T[:, kc, 512 * h:512 * h + 512], start=(kc == 0), stop=False)
                pe.wait_ge(s_xas, h + 1)
                mm(o[:, :], BT[:, oc * P:(oc + 1) * P], xaT[:, 512 * h:512 * h + 512], start=False, stop=True).then_inc(s_l1, 1)

            def project_kv(h):
                pe.wait_ge(s_x2, 2 * (h + 1))
                pe.wait_ge(s_xas, 2)
                for t in range(4 * h, 4 * h + 4):
                    for kc in range(KC):
                        i_ = mm(bank[1 + t // 2][:, (t % 2) * D:(t % 2) * D + D], x2T[:, kc, t * P:(t + 1) * P], WkvT[:, kc, :],
                                start=(kc == 0), stop=(kc == KC - 1))
                    if t % 2:
                        i_.then_inc(s_kvp, 1)

            pe.wait_ge(s_wtA, 2)
            layer1(0)
            pe.wait_ge(s_val, 1)
            hits = hit[0:NWI, :].rearrange("p (b j) -> p b j", j=WB)
            for j in range(WB):
                i_ = mm(bank[7][0:B, j * BLOCK:(j + 1) * BLOCK], hits[:, :, j], wr[0:NWI, 3, :], start=True, stop=True)
            i_.then_inc(s_nrow, 1)
            layer1(1)
            pe.wait_ge(s_xas, 2)
            turn_square(2, nat, 2, [(s_kvw, 32)])
            turn_square(3, nat, 1, [(s_qw, 16)])
            layer1(2)
            pe.wait_ge(s_wtA, 3)
            pe.wait_ge(s_wtD, 4)
            project_kv(0)
            pe.wait_ge(s_rowf, 1)
            tr(bank[7][:, 200:200 + B], rows[:, 1, 0:P], ident[0:B, 0:B])
            tr(bank[7][0:KB, 240:240 + B], rows[:, 1, P:KEYS], ident[0:B, 0:B]).then_inc(s_rowT, 1)
            layer1(3)
            project_kv(1)
            for t in range(NT):
                if t == 4:
                    pe.wait_ge(s_x2, 4)
                if t == 6:
                    pe.wait_ge(s_rowi, 5)
                for kc in range(KC):
                    i_ = mm(bank[(5, 6, 0, 7)[t // 2]][:, (t % 2) * D:(t % 2) * D + D], x2T[:, kc, t * P:(t + 1) * P],
                            WqT[:, kc, :, :].rearrange("p s c -> p (s c)"), start=(kc == 0), stop=(kc == KC - 1))
                if t % 2:
                    i_.then_inc(s_qp, 1)

            def turn_k(g):
                if g >= 1:
                    pe.wait_ge(s_kta, g)
                else:
                    pe.wait_ge(s_kvk, NT)
                for j in range(B4):
                    b = B4 * g + j
                    pe.wait_ge(s_kvA[b], 16)
                    i_ = tr(bank[1][:, j * P:(j + 1) * P], kvA(b, slice(0, KV)), ident)
                i_.then_inc(s_kt, 1)
                if g >= 1:
                    pe.wait_ge(s_qt, G * g)
                pe.wait_ge(s_kvB[g], 16)
                tr(bank[2][:, 0:P], kvB(g, slice(0, KV)), ident)
                pe.wait_ge(s_qready, g // 4 + 1)
                for s in range(GS):
                    i_ = tr(bank[2][:, P + s * P:P + (s + 1) * P], qn[:, g, s * KV:(s + 1) * KV], ident)
                i_.then_inc(s_kt, 1)

            def scores(n):
                g, j = divmod(n, B4)
                if j == 0:
                    pe.wait_ge(s_kta, g + 1)
                    pe.wait_ge(s_ktb, g + 1)
                    pe.wait_ge(s_qt, G * (g + 1))
                if n >= 2:
                    pe.wait_ge(s_mx, 2 * (n - 1))
                for u in range(2):
                    i_ = mm(bank[3 + n % 2][:, u * KEYS:(u + 1) * KEYS],
                            QBD[:, g % 2, j, 2 * u:2 * u + 2, :].rearrange("p g c -> p (g c)"), KT[:, g % 2, j, :],
                            start=True, stop=True)
                i_.then_inc(s_sc, 1)

            def turn_probs(seq):
                g, j = divmod(seq, B4 + 1)
                if j == 0:
                    pe.wait_ge(s_pb, B4 * (g + 1))
                else:
                    pe.wait_ge(s_pn, 2 * (B4 * g + j))
                if seq >= 2:
                    pe.wait_ge(s_pts, seq - 1)
                else:
                    pe.wait_ge(s_qk, 4)
                for u in range(2):
                    src = prB[:, g % 2, u, :, :].rearrange("p b r -> p (b r)") if j == 0 else pr[:, g % 2, u, j - 1, 0:P]
                    i_ = tr(bank[5 + seq % 2][:, u * P:(u + 1) * P], src, ident)
                i_.then_inc(s_pt, 1)

            def pv(n):
                g, j = divmod(n, B4)
                pe.wait_ge(s_pts, g * (B4 + 1) + j + 2)
                if j == 0:
                    if g:
                        pe.wait_ge(s_ot, g)
                    else:
                        pe.wait_ge(s_qk, 6)
                pe.wait_ge(s_vbd, g + 1)
                for k in range(G):
                    o = bank[0][HD * k:HD * k + HD, j * GS * T:(j + 1) * GS * T]
                    c = slice(GS * T * (k % 2), GS * T * (k % 2) + GS * T)
                    v = slice(KV + HD * k, KV + HD * k + HD)
                    mm(o, kvA(n, v), PTA[:, n % 3, k // 2, c], start=True, stop=False)
                    i_ = mm(o, VBD[:, g % 2, j, HD * k:HD * k + HD], PTB[:, g % 2, k // 2, c], start=False, stop=True)
                i_.then_inc(s_pv, 1)

            def project(g):
                pe.wait_ge(s_ot, g + 1)
                if g:
                    pe.wait_ge(s_res, g)
                else:
                    pe.wait_ge(s_qk, 8)
                for oc in range(KC):
                    for s in range(GS):
                        i_ = mm(bank[7][:, oc * P:(oc + 1) * P], WoT[:, s, oc * P:(oc + 1) * P], oT[:, g % 2, :, s, :],
                                start=(s == 0), stop=(s == GS - 1))
                i_.then_inc(s_wo, 1)

            def layer3(g):
                pe.wait_ge(s_x3, g + 1)
                o = bank[7][:, D:2 * D]
                for kc in range(KC):
                    mm(o[:, kc * P:(kc + 1) * P], x3T[:, g % 2, kc, :], ident, start=(kc == 0), stop=False, skip_group_check=True)
                for j in range(B4):
                    b = B4 * g + j
                    pe.wait_ge(s_we[b % NE], 16 * (b // NE + 1))
                    for kc in range(KC):
                        i_ = mm(o[T * j:T * j + T, :], x3T[:, g % 2, kc, T * j:T * j + T], We(b)[:, kc, :],
                                start=False, stop=(kc == KC - 1), skip_group_check=True)
                i_.then_inc(s_l3, 1)

            turn_k(0)
            scores(0)
            for n in range(B + TAIL):
                if n + 1 < B:
                    scores(n + 1)
                if n % B4 == 1 and n // B4 + 1 < NT:
                    turn_k(n // B4 + 1)
                m = n - TURN
                if 0 <= m < B:
                    if m % B4 == 0:
                        turn_probs(turned(m) - 2)
                    turn_probs(turned(m) - 1)
                if 0 <= n - PV < B:
                    pv(n - PV)
                k = n - PROJECT
                if 0 <= k < B and k % B4 == B4 - 1:
                    project(k // B4)
                k = n - LAYER3
                if 0 <= k < B and k % B4 == B4 - 1:
                    layer3(k // B4)


_INS = ["x", "itok_B_1_198", "itok_B_0_6", "itok_Bx257_0_4111", "itok_B_37_3939", "itok_B_0_15", "L0_cond_weights",
        "L1_cond_W", "L1_cond_A", "L1_cond_Bm", "L1_cond_scalings", "L2_cond_Wq", "L2_cond_Wk", "L2_cond_Wv",
        "L2_cond_Wo", "L2_cond_q_norm_scale", "L2_cond_k_norm_scale", "L2_cond_k_blocks", "L2_cond_v_blocks",
        "L3_cond_W", "L3_cond_b"]


def kernel(**inputs):
    from concourse import bacc
    from concourse.bass_utils import run_bass_kernel_spmd

    nc = bacc.Bacc("TRN2", target_bir_lowering=False, num_devices=1)
    arrays, args = {}, []
    for name in _INS:
        a = np.ascontiguousarray(inputs[name])
        arrays[f"in_{name}"] = a
        args.append(nc.dram_tensor(f"in_{name}", a.shape, mybir.dt.from_np(a.dtype), kind="ExternalInput").ap())
    c = Columns().data
    arrays["in_consts"] = c
    args.append(nc.dram_tensor("in_consts", c.shape, F32, kind="ExternalInput").ap())
    args.append(nc.dram_tensor("out", (B, T, D), F32, kind="ExternalOutput").ap())
    program(nc, *args)
    r = run_bass_kernel_spmd(nc, [arrays], core_ids=[0])
    return r.results[0]["out"]
```
